# Optimizing a Trainium2 kernel written in Bass

```python
import numpy as np
import jax
import jax.numpy as jnp

def _softmax(x, axis=-1):
    return jax.nn.softmax(x, axis=axis)

def _gelu(x):
    return jax.nn.gelu(x, approximate=True)

def _silu(x):
    return jax.nn.silu(x)

def _sigmoid(x):
    return jax.nn.sigmoid(x)

def _layernorm(x, axis=-1, eps=1e-05):
    m = jnp.mean(x, axis=axis, keepdims=True)
    v = jnp.var(x, axis=axis, keepdims=True)
    return (x - m) / jnp.sqrt(v + eps)

def _scatter_add(tgt, idx, src, axis=0):
    return tgt.at[idx].add(src)

def _segment_sum(src, seg, n):
    return jax.ops.segment_sum(src, seg, n)
kernel_name = 'mk_flamingo_gated_d1_seqx_r4_39e51c'

def setup_inputs(seed: int=0):
    np.random.seed(seed)
    _w = jnp.asarray

    def _rec_inputs():
        import jax
        import jax.numpy as jnp
        _rk = jax.random.key(seed)
        x = 0.0003765 + 1 * jax.random.normal(jax.random.fold_in(_rk, 1), (8, 256, 512), jnp.float32)
        _lenS = 256 - jax.random.randint(jax.random.fold_in(_rk, 7), (8,), 0, max(1, 256 // 4) + 1, jnp.int32)
        _lenS2 = 256 - jax.random.randint(jax.random.fold_in(_rk, 8), (8,), 0, max(1, 256 // 4) + 1, jnp.int32)
        _ctx_2048P = jax.random.normal(jax.random.fold_in(_rk, 11), (8, 16, 512), jnp.float32)
        _ctx_2048c = jax.random.dirichlet(jax.random.fold_in(_rk, 511), 0.3 * jnp.ones((16,), jnp.float32), (8, 256))
        _ctx_2048t = jnp.einsum('bsk,bkd->bsd', _ctx_2048c, _ctx_2048P)
        _ctx_2048t = _ctx_2048t * jax.lax.rsqrt(jnp.mean(jnp.square(_ctx_2048t)) + 1e-12) * 0.953939
        ctx_2048 = -0.000292821 + 1.00034 * (_ctx_2048t + 0.3 * jax.random.normal(jax.random.fold_in(_rk, 611), (8, 256, 512), jnp.float32))
        _g = jax.random.normal(jax.random.fold_in(_rk, 9001), (2, 1), jnp.float32)
        _g = jnp.sign(_g) * jnp.maximum(jnp.abs(_g), 1.0) + (_g == 0) * 1.0
        g_xattn = _g[0]
        g_ffn = _g[1]
        return (x, ctx_2048, g_xattn, g_ffn)
    x, ctx_2048, g_xattn, g_ffn = _rec_inputs()

    def _L0_xattn_setup():
        import jax, jax.numpy as jnp
        import numpy as np
        key = jax.random.key(seed)
        k1, k2, k3, k4, k5 = jax.random.split(key, 5)
        B, D_MODEL, L = (2, 256, 512)
        HEAD_DIM = 8
        H = D_MODEL // HEAD_DIM
        return {'k': jax.random.normal(k1, (B, D_MODEL, L), dtype=jnp.float32), 'v': jax.random.normal(k2, (B, D_MODEL, L), dtype=jnp.float32), 'q': jax.random.normal(k3, (B, D_MODEL, L), dtype=jnp.float32), 'ssm_kernel': jax.random.normal(k4, (H, L), dtype=jnp.float32), 'D': jax.random.normal(k5, (H,), dtype=jnp.float32), 'head_dim': HEAD_DIM}
    _L0_xattn_all = _L0_xattn_setup()
    _L0_xattn_in = {k: v for k, v in _L0_xattn_all.items() if k in ('ssm_kernel', 'D')}
    del _L0_xattn_all

    def _L0_ffn_setup():
        import jax, jax.numpy as jnp
        import numpy as np
        DIM = 512
        INTER = 352
        N_EXPERTS = 16
        TOP_K = 2
        N_SHARED = 2
        SHARED_INTER = N_SHARED * INTER

        def _swiglu(t, wa, wb, wo):
            h = jax.nn.silu(t @ wa.T) * (t @ wb.T)
            return h @ wo.T
        key = jax.random.key(seed)
        ks = jax.random.split(key, 9)
        s = 0.02
        return {'x': jax.random.normal(ks[0], (4, 512, DIM), dtype=jnp.float32), 'gate_w': jax.random.normal(ks[1], (N_EXPERTS, DIM), dtype=jnp.float32) * s, 'w1': jax.random.normal(ks[2], (N_EXPERTS, INTER, DIM), dtype=jnp.float32) * s, 'w2': jax.random.normal(ks[3], (N_EXPERTS, DIM, INTER), dtype=jnp.float32) * s, 'w3': jax.random.normal(ks[4], (N_EXPERTS, INTER, DIM), dtype=jnp.float32) * s, 'sw1': jax.random.normal(ks[5], (SHARED_INTER, DIM), dtype=jnp.float32) * s, 'sw2': jax.random.normal(ks[6], (DIM, SHARED_INTER), dtype=jnp.float32) * s, 'sw3': jax.random.normal(ks[7], (SHARED_INTER, DIM), dtype=jnp.float32) * s}
    _L0_ffn_all = _L0_ffn_setup()
    _L0_ffn_in = {k: v for k, v in _L0_ffn_all.items() if k in ('gate_w', 'w1', 'w2', 'w3', 'sw1', 'sw2', 'sw3')}
    del _L0_ffn_all
    return {'x': x, 'ctx_2048': ctx_2048, 'g_xattn': g_xattn, 'g_ffn': g_ffn, 'L0_xattn_ssm_kernel': _L0_xattn_in['ssm_kernel'], 'L0_xattn_D': _L0_xattn_in['D'], 'L0_ffn_gate_w': _L0_ffn_in['gate_w'], 'L0_ffn_w1': _L0_ffn_in['w1'], 'L0_ffn_w2': _L0_ffn_in['w2'], 'L0_ffn_w3': _L0_ffn_in['w3'], 'L0_ffn_sw1': _L0_ffn_in['sw1'], 'L0_ffn_sw2': _L0_ffn_in['sw2'], 'L0_ffn_sw3': _L0_ffn_in['sw3']}

def reference(x, ctx_2048, g_xattn, g_ffn, L0_xattn_ssm_kernel, L0_xattn_D, L0_ffn_gate_w, L0_ffn_w1, L0_ffn_w2, L0_ffn_w3, L0_ffn_sw1, L0_ffn_sw2, L0_ffn_sw3):
    import jax
    import jax.numpy as jnp

    def _L0_xattn_ref(k, v, q, ssm_kernel, D, head_dim):
        import jax, jax.numpy as jnp
        import numpy as np
        B, HD, L = k.shape
        H = HD // head_dim
        fft_size = 2 * L
        k_ = k.reshape(B, H, head_dim, L)
        v_ = v.reshape(B, H, head_dim, L)
        q_ = q.reshape(B, H, head_dim, L)
        kv = jnp.einsum('bhil,bhjl->bijhl', k_, v_)
        kv_f = jnp.fft.rfft(kv, n=fft_size)
        kernel_f = jnp.fft.rfft(ssm_kernel, n=fft_size)
        y = jnp.fft.irfft(kv_f * kernel_f, n=fft_size)[..., :L]
        out = y + kv * D[None, None, None, :, None]
        out = jnp.einsum('bijhl,bhil->bjhl', out, q_)
        out = jnp.transpose(out, (0, 2, 1, 3)).reshape(B, H * head_dim, L)
        return out.astype(k.dtype)

    def _L0_ffn_ref(x, gate_w, w1, w2, w3, sw1, sw2, sw3):
        import jax, jax.numpy as jnp
        import numpy as np
        DIM = 512
        INTER = 352
        N_EXPERTS = 16
        TOP_K = 2
        N_SHARED = 2
        SHARED_INTER = N_SHARED * INTER

        def _swiglu(t, wa, wb, wo):
            h = jax.nn.silu(t @ wa.T) * (t @ wb.T)
            return h @ wo.T
        shape = x.shape
        t = x.reshape(-1, DIM)
        scores = jax.nn.softmax(t @ gate_w.T, axis=-1)
        weights, indices = jax.lax.top_k(scores, TOP_K)
        y = jnp.zeros_like(t)
        for e in range(N_EXPERTS):
            w_e = jnp.sum(jnp.where(indices == e, weights, 0.0), axis=-1)
            y = y + _swiglu(t, w1[e], w3[e], w2[e]) * w_e[:, None]
        z = _swiglu(t, sw1, sw3, sw2)
        return (y + z).reshape(shape)
    x = x + jnp.tanh(g_xattn[0]) * _L0_xattn_ref(ctx_2048, ctx_2048, _layernorm(x, axis=-1), L0_xattn_ssm_kernel, L0_xattn_D, 8)
    x = x + jnp.tanh(g_ffn[0]) * _L0_ffn_ref(_layernorm(x, axis=-1), L0_ffn_gate_w, L0_ffn_w1, L0_ffn_w2, L0_ffn_w3, L0_ffn_sw1, L0_ffn_sw2, L0_ffn_sw3)
    return x

_drawn_inputs = setup_inputs


def setup_inputs(seed=0):
    import zlib

    import numpy as np

    out = dict(_drawn_inputs(seed))
    spreads = {}
    factors = {'L0_ffn_gate_w': 8.0,
     'L0_ffn_w1': 8.0,
     'L0_ffn_w2': 8.0,
     'L0_ffn_w3': 8.0,
     'L0_ffn_sw1': 8.0,
     'L0_ffn_sw2': 8.0,
     'L0_ffn_sw3': 8.0}
    for name, (base, spread) in spreads.items():
        noise = np.random.default_rng([zlib.crc32(name.encode()), seed]).standard_normal(out[name].shape)
        drawn = base * np.exp(spread * noise) if base else spread * noise
        out[name] = jnp.asarray(drawn.astype(out[name].dtype))
    for name, factor in factors.items():
        out[name] = (out[name] * factor).astype(out[name].dtype)
    return out
```

```python
from contextlib import ExitStack

import concourse.bass as bass
from concourse import mybir

F32 = mybir.dt.float32
F32R = mybir.dt.float32r
BF16 = mybir.dt.bfloat16
I32 = mybir.dt.int32
U32 = mybir.dt.uint32
ALU = mybir.AluOpType
ACT = mybir.ActivationFunctionType
AX = mybir.AxisListType

P = 128
BATCH, HEADS, HD, L = 8, 32, 8, 512
ROWS = BATCH * HEADS * HD
TILES = ROWS // P
BLOCKS = L // P
PAIRS = HD * (HD + 1) // 2
EXT = HD + HD // 2
GROUPS = 2 * BATCH
SUMROWS = 9
EXPERTS, INTER = 16, 352
SHARED = 2
W13 = BLOCKS * 2 * INTER
ICH = (INTER + P - 1) // P
IPAD = ICH * P
W2 = ICH * L
WROW = W13 + W2
HALF = W13 // 2
UNITS2 = SHARED * TILES
SLOT_TILES = (2 * ROWS + EXPERTS * (P - 1)) // P
SLOTS = SLOT_TILES + 1
STAGE = SHARED * WROW // TILES
EPS = 1e-5
SKIP = 1 << 20
FIELDS = 6


class At:

    def __init__(self, b, a=0, i=None, n=1):
        self.a, self.b, self.i, self.n = (a, b, i, n) if i is not None else (0, b, None, 1)

    def __add__(self, k):
        return At(self.b + k, self.a, self.i, self.n)

    def __sub__(self, k):
        return self + (-k)

    def __mul__(self, k):
        return At(self.b * k, self.a * k, self.i, self.n)

    def half(self):
        assert self.a % 2 == 0
        return At(self.b // 2, self.a // 2, self.i, self.n)

    @property
    def odd(self):
        assert self.a % 2 == 0
        return self.b % 2

    def within(self, low, high):
        ends = {low <= self.b < high, low <= self.b + self.a * (self.n - 1) < high}
        assert len(ends) == 1
        return ends.pop()

    @property
    def v(self):
        return self.b if self.i is None else self.i * self.a + self.b


def wait(eng, sem, count):
    count = count if isinstance(count, At) else At(count)
    if count.i is None and count.b <= 0:
        return
    assert count.b > 0
    eng.wait_ge(sem, count.v)


def view(ap, offset, dims):
    return bass.AP(ap.tensor, ap.offset + offset, [list(ap.ap[0])] + dims)


def program(nc, x, ctx_ext, conv_rows, conv_d, gates, gate_w, weights, out):
    ctx = ExitStack()
    with ctx:
        def sem(name):
            return ctx.enter_context(nc.semaphore(name))

        def sem2(name):
            return [sem(name + "0"), sem(name + "1")]

        def sb(name, shape, dt=F32, stack=ctx):
            return stack.enter_context(nc.sbuf_tensor(name, shape, dt))

        def sb2(name, shape, dt=F32, stack=ctx):
            return [sb(name + "0", shape, dt, stack), sb(name + "1", shape, dt, stack)]

        kpad = nc.dram_tensor("kpad", (HEADS, 640), F32, kind="Internal").ap()
        x2_rows = nc.dram_tensor("x2_rows", (ROWS, L), F32, kind="Internal").ap()
        t_rows = nc.dram_tensor("t_rows", (ROWS, L), F32, kind="Internal").ap()
        toeplitz = bass.AP(kpad.tensor, 0, [[2 * 640, TILES], [1, P], [640, 2], [1, L]])
        x_t = x.rearrange("(t p) l -> t p l", p=P)
        x2_t = x2_rows.rearrange("(t p) l -> t p l", p=P)
        t_t = t_rows.rearrange("(t p) l -> t p l", p=P)
        out_t = out.rearrange("(t p) l -> t p l", p=P)

        bank = [ctx.enter_context(nc.psum_tensor(f"bank{n}", [P, 512], F32)) for n in range(8)]
        ps_conv = [[bank[0], bank[1]], [bank[2], bank[3]]]
        ps_o, ps_q, ps_t, ps_gate = bank[4], bank[5], bank[6], bank[7]
        ps_h1, ps_h3, ps_ht, ps_y = bank[0], bank[1], bank[2], bank[3]
        ps_rank, ps_total, ps_table = bank[4], bank[5], bank[7]

        ident = sb("ident", [P, P])
        small = sb("small", [P, 8])
        gts = sb("gts", [P, 2])
        hop, phop = sb("hop", [P, 2]), sb("phop", [P, 5])
        gw = sb("gw", [P, BLOCKS * EXPERTS])
        raw = sb("raw", [P, WROW])
        shared_hi = sb("shared_hi", [P, SHARED * WROW], F32R)
        shared_lo = sb("shared_lo", [P, SHARED * WROW], F32R)
        tn = sb2("tn", [P, L])
        x2in = sb2("x2in", [P, L])
        tT_hi = sb2("tT_hi", [P, L], F32R)
        tT_lo = sb2("tT_lo", [P, L], F32R)
        silu = sb("silu", [P, INTER])
        hid = sb2("hid", [P, IPAD])
        hT_hi = sb2("hT_hi", [P, IPAD], F32R)
        hT_lo = sb2("hT_lo", [P, IPAD], F32R)
        ys = sb2("ys", [P, L])
        logits = sb("logits", [P, TILES * EXPERTS])
        slot_info = sb("slot_info", [P, 3 * SLOTS], I32)
        tile_info = sb("tile_info", [P, 2 * SLOTS], I32)
        gat_i = sb2("gat_i", [P, 3], I32)
        sca_i = sb2("sca_i", [P, 3], I32)

        one = ExitStack()
        cx = sb2("cx", [P, BLOCKS * GROUPS * EXT], F32, one)
        toep = sb2("toep", [P, 2 * L], F32, one)
        kv = sb2("kv", [P, BLOCKS * GROUPS * PAIRS], F32, one)
        xt = sb2("xt", [P, L], F32, one)
        xr = sb2("xr", [P, L], F32, one)
        xn = sb2("xn", [P, L], F32, one)
        q = sb2("q", [P, BLOCKS * GROUPS * EXT], F32, one)
        prod = sb2("prod", [P, SUMROWS * P], F32, one)
        tT = sb("tT", [P, L], F32, one)
        x2 = sb2("x2", [P, L], F32, one)
        st1, st2 = sb2("st1_", [P, 6], F32, one), sb2("st2_", [P, 6], F32, one)
        mv1, mv2 = sb2("mv1_", [P, 2], F32, one), sb2("mv2_", [P, 2], F32, one)
        sd1, sd2 = sb2("sd1_", [P, 2], F32, one), sb2("sd2_", [P, 2], F32, one)
        krow = sb("krow", [HEADS, 640], F32, one)
        drow = sb("drow", [HEADS, 1], F32, one)
        one.close()
        w_hi = [sb("w_hi0", [P, WROW], F32R)]
        w_lo = [sb("w_lo0", [P, WROW], F32R)]
        route = ExitStack()
        io = sb("io", [P, P], F32, route)
        iob = sb("iob", [P, P], BF16, route)
        upper = sb("upper", [P, P], BF16, route)
        ones = sb("ones", [P, P], BF16, route)
        mx = sb("mx", [P, TILES, 8], F32, route)
        mi = sb("mi", [P, TILES, 8], U32, route)
        pick = sb("pick", [P, 2, TILES], F32, route)
        mask = [sb(f"mask{k}", [P, TILES, EXPERTS], F32, route) for k in range(2)]
        both = sb("both", [P, TILES, EXPERTS], BF16, route)
        lex = sb("lex", [P, TILES, EXPERTS + 1], F32, route)
        ssum = sb("ssum", [P, TILES], F32, route)
        wts = sb("wts", [P, 2, TILES], F32, route)
        wres = sb("wres", [P, 2 * TILES], F32, route)
        wpart = sb("wpart", [P, 3, 2 * TILES], BF16, route)
        cum = sb2("cum", [P, TILES, EXPERTS], F32, route)
        cmp = sb("cmp", [P, EXPERTS, TILES], F32, route)
        ntile = sb2("ntile", [P, EXPERTS], F32, route)
        ntile0 = sb("ntile_own", [P, EXPERTS], F32, route)
        slot = sb("slot", [P, 2 * TILES], F32, route)
        sloti = sb("sloti", [P, 3, 2 * TILES], I32, route)
        slotb = sb("slotb", [P, 2, 2 * TILES], BF16, route)
        prow = sb("prow", [P, 2 * TILES], BF16, route)
        trow = sb("trow", [P, 2 * TILES], BF16, route)
        place = sb("place", [P, 2 * TILES, P], BF16, route)
        field = sb("field", [P, 2 * TILES, FIELDS, SLOTS], BF16, route)
        tab = sb("tab", [P, FIELDS, SLOTS], F32, route)
        tcmp = sb("tcmp", [P, SLOTS, EXPERTS], F32, route)
        texp = sb("texp", [P, SLOTS + 1], F32, route)
        tmpf = sb("tmpf", [P, SLOTS], F32, route)
        pid = sb("pid", [P, 1], F32, route)
        route.close()
        w_hi.append(sb("w_hi1", [P, WROW], F32R))
        w_lo.append(sb("w_lo1", [P, WROW], F32R))

        consts_in, kpad_in, kpad_ok, kpad_out = sem("consts_in"), sem("kpad_in"), sem("kpad_ok"), sem("kpad_out")
        setup_dve, setup_pool, gate_tanh = sem("setup_dve"), sem("setup_pool"), sem("gate_tanh")
        x_in, xr_in, ctx_in, toep_in, stage_in = (sem2(n) for n in ("x_in", "xr_in", "ctx_in", "toep_in", "stage_in"))
        stat1, std1, rstd1, xn_ok = sem("stat1"), sem("std1"), sem("rstd1"), sem("xn_ok")
        q_turned, q_ok, kv_ok = sem("q_turned"), sem("q_ok"), sem("kv_ok")
        conv_ok, prod_ok, summed = sem("conv_ok"), sem("prod_ok"), sem("summed")
        x2_ok, stat2, std2, rstd2, t_ok = sem("x2_ok"), sem("stat2"), sem("std2"), sem("rstd2"), sem("t_ok")
        t_turned, tT_ok, gate_ok, logits_ok = sem("t_turned"), sem("tT_ok"), sem("gate_ok"), sem("logits_ok")
        shi_ok, slo_ok = sem("shi_ok"), sem("slo_ok")
        x2_out, t_out = sem2("x2_out"), sem2("t_out")
        rt, r_const, r_exp, r_count, r_table = sem("rt"), sem("r_const"), sem("r_exp"), sem("r_count"), sem("r_table")
        r_both, r_fields, r_done = sem("r_both"), sem("r_fields"), sem("r_done")
        tn_in, x2_in, row_in = sem2("tn_in"), sem2("x2_in"), sem2("row_in")
        tile_turned, tTh_ok, tTl_ok = sem("tile_turned"), sem("tTh_ok"), sem("tTl_ok")
        up_ok, silu_ok, hid_ok = sem("up_ok"), sem("silu_ok"), sem("hid_ok")
        hid_turned, hTh_ok, hTl_ok, down_ok = sem("hid_turned"), sem("hTh_ok"), sem("hTl_ok"), sem("down_ok")
        y_ok, yr_ok, out_ok = sem("y_ok"), sem("yr_ok"), sem2("out_ok")
        raw_in = [sem("rawA_in"), sem("rawB_in"), sem("rawC_in")]
        hi_ok = [sem("hiA_ok"), sem("hiB_ok"), sem("hiC_ok")]
        lo_ok = [sem("loA_ok"), sem("loB_ok"), sem("loC_ok")]
        gidx_ok, sidx_ok, added, hid_zero = sem("gidx_ok"), sem("sidx_ok"), sem2("added"), sem("hid_zero")
        PIECE = [(0, HALF), (HALF, W13), (W13, WROW)]

        block = ctx.enter_context(nc.Block())

        def pairs(eng, turn):
            for t in range(3):
                turn(At(t))
            n = (TILES - 4) // 2
            with eng.Fori(0, n) as i:
                for o in (3, 4):
                    turn(At(o, 2, i, n))
            turn(At(TILES - 1))

        LOOP2 = (16, 3)
        LOOP3 = (6, 19)
        LAST = SLOT_TILES + 3

        def steps(eng, step, after=lambda u: None):
            for u in range(-1, LOOP2[0]):
                step(At(u))
                after(u)
            with eng.Fori(0, LOOP2[1]) as i:
                for o in range(4):
                    step(At(LOOP2[0] + o, 4, i, LOOP2[1]))
            for u in range(LOOP2[0] + 4 * LOOP2[1], UNITS2 + LOOP3[0]):
                step(At(u))
            with eng.Fori(0, LOOP3[1]) as i:
                for o in range(2):
                    step(At(UNITS2 + LOOP3[0] + o, 2, i, LOOP3[1]))
            for u in range(UNITS2 + LOOP3[0] + 2 * LOOP3[1], UNITS2 + LAST):
                step(At(u))

        def shared(u):
            return u.within(0, UNITS2)

        def routed(u):
            return u.within(UNITS2, UNITS2 + SLOT_TILES)

        def tile_of(u):
            return u.half() if shared(u) else u - TILES

        def turned_at(u):
            if u.within(-1, 0):
                return [At(0)]
            if shared(u) and not u.odd:
                return [u.half() + 1]
            if u.within(UNITS2 - 1, UNITS2):
                return [At(TILES + 1)]
            if routed(u) and routed(u + 2):
                return [tile_of(u + 2)]
            return []

        R_PICK = 2 + 2 * TILES
        R_EXP = R_PICK + 7

        @block.sync
        def _(sp):
            sp.wait_ge(setup_dve, 1)
            sp.dma_start(krow[:, P - 1:P - 1 + L], conv_rows).then_inc(kpad_in, 16)
            sp.dma_start(drow[:], conv_d).then_inc(kpad_in, 16)
            sp.dma_start(xt[0][:], x_t[0]).then_inc(x_in[0], 16)
            sp.dma_start(cx[0][:], ctx_ext[0]).then_inc(ctx_in[0], 16)
            sp.dma_start(gts[:], gates).then_inc(consts_in, 16)
            sp.dma_start(gw[:], gate_w).then_inc(consts_in, 16)
            sp.dma_start(xt[1][:], x_t[1]).then_inc(x_in[1], 16)
            sp.dma_start(cx[1][:], ctx_ext[1]).then_inc(ctx_in[1], 16)
            sp.wait_ge(kpad_ok, 1)
            sp.dma_start(kpad, krow[:]).then_inc(kpad_out, 16)
            sp.wait_ge(kpad_out, 16)
            shared_t = bass.AP(weights.tensor, EXPERTS * P * WROW, [[P * STAGE, TILES], [STAGE, P], [1, STAGE]])

            def load(t, which):
                p = t.odd
                if which == "toep":
                    sp.dma_start(toep[p][:].rearrange("p (h c) -> p h c", h=2),
                                 toeplitz[bass.ds(t.v, 1)].rearrange("x p h c -> (x p) h c")).then_inc(toep_in[p], 16)
                if which == "ctx":
                    sp.dma_start(cx[p][:], ctx_ext[bass.ds(t.v, 1)].rearrange("x p c -> (x p) c")).then_inc(ctx_in[p], 16)
                if which == "x":
                    sp.dma_start(xt[p][:], x_t[bass.ds(t.v, 1)].rearrange("x p c -> (x p) c")).then_inc(x_in[p], 16)
                if which == "xr":
                    sp.dma_start(xr[p][:], x_t[bass.ds(t.v, 1)].rearrange("x p c -> (x p) c")).then_inc(xr_in[p], 16)
                if which == "stage":
                    sp.dma_start(raw[:, p * STAGE:(p + 1) * STAGE],
                                 shared_t[bass.ds(t.v, 1)].rearrange("x p c -> (x p) c")).then_inc(stage_in[p], 16)

            for t in (At(0), At(1)):
                load(t, "toep")
            for t in (At(0), At(1)):
                load(t, "xr")
                load(t, "stage")

            def turn(t, ahead=True):
                p = t.odd
                if ahead:
                    wait(sp, kv_ok, (t + 1) * 2)
                    load(t + 2, "ctx")
                    wait(sp, xn_ok, t + 1)
                    load(t + 2, "x")
                    wait(sp, slo_ok, t + 1)
                    load(t + 2, "stage")
                    wait(sp, conv_ok, (t + 1) * 8)
                    load(t + 2, "toep")
                wait(sp, x2_ok, t + 1)
                sp.dma_start(x2_t[bass.ds(t.v, 1)].rearrange("x p c -> (x p) c"), x2[p][:]).then_inc(x2_out[p], 16)
                if ahead:
                    load(t + 2, "xr")
                wait(sp, t_ok, t + 1)
                sp.dma_start(t_t[bass.ds(t.v, 1)].rearrange("x p c -> (x p) c"), tn[p][:]).then_inc(t_out[p], 16)

            n = (TILES - 2) // 2
            with sp.Fori(0, n) as i:
                turn(At(0, 2, i, n))
                turn(At(1, 2, i, n))
            turn(At(TILES - 2), False)
            turn(At(TILES - 1), False)
            for p in (0, 1):
                sp.wait_ge(x2_out[p], 16 * TILES // 2)
                sp.wait_ge(t_out[p], 16 * TILES // 2)

            def load_rows(j):
                p = j.odd
                wait(sp, tile_turned, j - 1)
                sp.dma_start(tn[p][:], t_t[bass.ds(j.v, 1)].rearrange("x p c -> (x p) c")).then_inc(tn_in[p], 16)
                wait(sp, y_ok, j - 1)
                sp.dma_start(x2in[p][:], x2_t[bass.ds(j.v, 1)].rearrange("x p c -> (x p) c")).then_inc(x2_in[p], 16)

            def store_rows(j):
                p = j.odd
                wait(sp, y_ok, j + 1)
                sp.dma_start(out_t[bass.ds(j.v, 1)].rearrange("x p c -> (x p) c"), ys[p][:]).then_inc(out_ok[p], 16)

            def load_weights(s, pieces):
                info = [sp.value_load(tile_info[0:1, bass.ds(s.v * 2 + k, 1)], min_val=0,
                                      max_val=[(EXPERTS - 1) * P, 1][k]) for k in (0, 1)]
                for n_ in pieces:
                    a, b = PIECE[n_]
                    wait(sp, lo_ok[n_], s)
                    sp.dma_start(raw[:, a:b], weights[bass.ds(info[0], P), a:b],
                                 cond=(info[1] > 0)).then_inc(raw_in[n_], 16)

            sp.wait_ge(t_turned, TILES)
            load_rows(At(0))
            load_rows(At(1))

            def step(u):
                if shared(u) and u.odd and shared(u - 3) and u.within(3, UNITS2):
                    store_rows((u - 3).half())
                if u.within(UNITS2, UNITS2 + 2) and u.odd:
                    store_rows(At(TILES - 1))
                if u.within(0, UNITS2 - 2 * 2) and u.odd:
                    load_rows((u - 1).half() + 2)
                if u.within(UNITS2 - 2, UNITS2 - 1):
                    sp.wait_ge(r_done, 1)
                    sp.wait_ge(slo_ok, TILES)
                if routed(u + 2):
                    load_weights(u + 2 - UNITS2, (0, 1))
                if routed(u):
                    load_weights(u - UNITS2, (2,))

            steps(sp, step)
            for p in (0, 1):
                sp.wait_ge(added[p], 16 * ((SLOT_TILES + 1 - p) // 2))
                sp.wait_ge(out_ok[p], 16 * TILES // 2)

        @block.scalar
        def _(act):
            act.wait_ge(consts_in, 32)
            act.activation(small[:, 1:3], gts[:], ACT.Tanh).then_inc(gate_tanh, 1)
            act.wait_ge(setup_dve, 2)

            def std_x(t):
                wait(act, stat1, (t + 1) * 2)
                act.activation(sd1[t.odd][:, 0:1], mv1[t.odd][:, 1:2], ACT.Sqrt, bias=small[:, 0:1]).then_inc(std1, 1)

            def std_x2(t):
                wait(act, stat2, (t + 1) * 2)
                act.activation(sd2[t.odd][:, 0:1], mv2[t.odd][:, 1:2], ACT.Sqrt, bias=small[:, 0:1]).then_inc(std2, 1)

            def q_copy(t):
                p = t.odd
                wait(act, prod_ok, (t - 1) * 24)
                wait(act, q_turned, t + 1)
                src = ps_q[:].rearrange("p (l c) -> p l c", l=BLOCKS)
                dst = q[p][:].rearrange("p (l c) -> p l c", l=BLOCKS)
                act.activation(dst[:, :, 0:P], src, ACT.Copy).then_inc(q_ok, 1)
                act.activation(dst[:, :, P:], src[:, :, 0:GROUPS * EXT - P], ACT.Copy).then_inc(q_ok, 1)

            def tT_copy(t):
                wait(act, t_turned, t + 1)
                wait(act, gate_ok, t)
                act.activation(tT[:], ps_t[:], ACT.Copy).then_inc(tT_ok, 1)

            def split_shared(t):
                p = t.odd
                wait(act, stage_in[p], (t.half() + 1) * 16)
                act.activation(shared_hi[:, bass.ds(t.v * STAGE, STAGE)],
                               raw[:, p * STAGE:(p + 1) * STAGE], ACT.Copy).then_inc(shi_ok, 1)

            std_x(At(0))
            q_copy(At(0))

            def turn(t):
                if not t.within(0, 1):
                    std_x2(t - 1)
                if not t.within(TILES - 1, TILES):
                    std_x(t + 1)
                split_shared(t)
                if not t.within(0, 1):
                    tT_copy(t - 1)
                if not t.within(TILES - 1, TILES):
                    q_copy(t + 1)

            pairs(act, turn)
            std_x2(At(TILES - 1))
            tT_copy(At(TILES - 1))

            def tile_hi(j):
                wait(act, tile_turned, j + 1)
                act.activation(tT_hi[j.odd][:], ps_t[:], ACT.Copy).then_inc(tTh_ok, 1)

            def step(u):
                s = u - UNITS2
                if routed(u - 3):
                    v = u - 3
                    wait(act, down_ok, v + 1)
                    wait(act, added[v.odd], (v - UNITS2).half() * 16)
                    wait(act, sidx_ok, v - UNITS2 + 1)
                    act.activation(ys[v.odd][:], ps_y[:], ACT.Copy,
                                   scale=sca_i[v.odd][:, 2:3].bitcast(F32)).then_inc(yr_ok, 1)
                if routed(u + 1):
                    v = u + 1
                    for n_ in (0, 1):
                        a, b = PIECE[n_]
                        wait(act, raw_in[n_], (v - UNITS2 + 1) * 16)
                        wait(act, up_ok, v - 1)
                        act.activation(w_hi[v.odd][:, a:b], raw[:, a:b], ACT.Copy).then_inc(hi_ok[n_], 1)
                if shared(u) or routed(u):
                    wait(act, hid_ok, u)
                    wait(act, up_ok, u + 1)
                    act.activation(silu[:], ps_h1[:, 0:INTER], ACT.Silu).then_inc(silu_ok, 1)
                v = u - 1
                if shared(v) or routed(v):
                    wait(act, down_ok, v - 1)
                    wait(act, hid_turned, v + 1)
                    act.activation(hT_hi[v.odd][:], ps_ht[:, 0:IPAD], ACT.Copy).then_inc(hTh_ok, 1)
                for j in turned_at(u):
                    tile_hi(j)

            def after(u):
                if u == 4:
                    act.wait_ge(rt, R_EXP)
                    act.activation(lex[:], lex[:], ACT.Exp).then_inc(r_exp, 1)

            steps(act, step, after)

        @block.vector
        def _(dve):
            dve.memset(krow[:], 0.0).then_inc(setup_dve, 1)
            dve.memset(small[:, 0:1], EPS).then_inc(setup_dve, 1)
            dve.memset(hop[:], 0.0).then_inc(setup_dve, 1)
            dve.wait_ge(kpad_in, 32)
            dve.tensor_tensor(krow[:, P - 1:P], krow[:, P - 1:P], drow[:], ALU.add).then_inc(kpad_ok, 1)
            dve.memset(prod[0][:], 0.0).then_inc(setup_dve, 1)
            dve.memset(prod[1][:], 0.0).then_inc(setup_dve, 1)
            dve.memset(hid[0][:, INTER:IPAD], 0.0).then_inc(hid_zero, 1)
            dve.memset(hid[1][:, INTER:IPAD], 0.0).then_inc(hid_zero, 1)
            dve.wait_ge(setup_dve, 5)

            def stats(src, st, mv, ok, t):
                p = t.odd
                dve.bn_stats(st[p][:], src[p][:]).then_inc(ok, 1)
                wait(dve, ok, t * 2 + 1)
                dve.tensor_copy(hop[:, 1:2], hop[:, 0:1])
                dve.bn_aggr(mv[p][:], st[p][:]).then_inc(ok, 1)

            def stats_x(t):
                dve.wait_ge(setup_dve, 1)
                wait(dve, x_in[t.odd], (t.half() + 1) * 16)
                stats(xt, st1, mv1, stat1, t)

            def norm_x(t):
                p = t.odd
                wait(dve, std1, t + 1)
                dve.reciprocal(sd1[p][:, 1:2], sd1[p][:, 0:1]).then_inc(rstd1, 1)
                wait(dve, q_turned, t - 1)
                wait(dve, rstd1, t + 1)
                dve.tensor_scalar(xn[p][:], xt[p][:], mv1[p][:, 0:1], sd1[p][:, 1:2],
                                  ALU.subtract, ALU.mult).then_inc(xn_ok, 1)

            def residual(t):
                p = t.odd
                wait(dve, x2_out[p], t.half() * 16)
                wait(dve, xr_in[p], (t.half() + 1) * 16)
                wait(dve, summed, (t + 1) * 4)
                dve.scalar_tensor_tensor(x2[p][:], ps_o[:], small[:, 1:2], xr[p][:],
                                         ALU.mult, ALU.add).then_inc(x2_ok, 1)
                wait(dve, x2_ok, t + 1)
                stats(x2, st2, mv2, stat2, t)

            def norm_x2(t):
                p = t.odd
                wait(dve, std2, t + 1)
                dve.reciprocal(sd2[p][:, 1:2], sd2[p][:, 0:1]).then_inc(rstd2, 1)
                wait(dve, t_out[p], t.half() * 16)
                wait(dve, t_turned, t - 1)
                wait(dve, rstd2, t + 1)
                dve.tensor_scalar(tn[p][:], x2[p][:], mv2[p][:, 0:1], sd2[p][:, 1:2],
                                  ALU.subtract, ALU.mult).then_inc(t_ok, 1)

            def products(t, lb):
                par = lb % 2
                G, HB = GROUPS, HD * BATCH
                for h in range(2):
                    y = ps_conv[par][h][:]
                    qo = lb * GROUPS * EXT + h * BATCH
                    po = h * BATCH
                    qq, pp = q[t.odd][:], prod[par][:]
                    if h == 0:
                        wait(dve, summed, t * 4 + lb - 1)
                        if lb == 0:
                            wait(dve, q_ok, (t + 1) * 2)
                    wait(dve, conv_ok, t * 8 + 2 * lb + h + 1)
                    dve.tensor_tensor(view(pp, po, [[P + G, 4], [G, HD], [1, BATCH]]),
                                      view(y, 0, [[HB, 4], [BATCH, HD], [1, BATCH]]),
                                      view(qq, qo, [[0, 4], [G, HD], [1, BATCH]]), ALU.mult).then_inc(prod_ok, 1)
                    dve.tensor_tensor(view(pp, po + 5 * P, [[P, 3], [G, HD], [1, BATCH]]),
                                      view(y, HB, [[HB, 3], [BATCH, HD], [1, BATCH]]),
                                      view(qq, qo + G, [[G, 3], [G, HD], [1, BATCH]]), ALU.mult).then_inc(prod_ok, 1)
                    dve.tensor_tensor(view(pp, po + 8 * P, [[4 * G, 2], [G, 4], [1, BATCH]]),
                                      view(y, 4 * HB, [[0, 2], [BATCH, 4], [1, BATCH]]),
                                      view(qq, qo + 4 * G, [[4 * G, 2], [G, 4], [1, BATCH]]), ALU.mult).then_inc(prod_ok, 1)

            def logits_copy(t):
                wait(dve, gate_ok, t + 1)
                dve.tensor_scalar(logits[:, bass.ds(t.v * EXPERTS, EXPERTS)], ps_gate[:, 0:EXPERTS], 1.0, None,
                                  ALU.mult).then_inc(logits_ok, 1)

            stats_x(At(0))
            norm_x(At(0))
            dve.wait_ge(gate_tanh, 1)

            def turn(t):
                first, last = t.within(0, 1), t.within(TILES - 1, TILES)
                products(t, 0)
                if not first:
                    residual(t - 1)
                if not last:
                    stats_x(t + 1)
                products(t, 1)
                if not first:
                    norm_x2(t - 1)
                if not last:
                    norm_x(t + 1)
                products(t, 2)
                products(t, 3)
                if not first:
                    logits_copy(t - 1)

            pairs(dve, turn)
            residual(At(TILES - 1))
            norm_x2(At(TILES - 1))

            def tile_lo(j):
                wait(dve, tTh_ok, j + 1)
                dve.tensor_tensor(tT_lo[j.odd][:], ps_t[:], tT_hi[j.odd][:].bitcast(F32),
                                  ALU.subtract).then_inc(tTl_ok, 1)

            dve.wait_ge(hid_zero, 2)

            def step(u):
                if routed(u - 1):
                    v = u - 1
                    a, b = PIECE[2]
                    wait(dve, raw_in[2], (v - UNITS2 + 1) * 16)
                    wait(dve, down_ok, v - 1)
                    dve.tensor_copy(w_hi[v.odd][:, a:b], raw[:, a:b]).then_inc(hi_ok[2], 1)
                if routed(u + 1):
                    v = u + 1
                    for n_ in (0, 1):
                        a, b = PIECE[n_]
                        wait(dve, hi_ok[n_], v - UNITS2 + 1)
                        dve.tensor_tensor(w_lo[v.odd][:, a:b], raw[:, a:b], w_hi[v.odd][:, a:b].bitcast(F32),
                                          ALU.subtract).then_inc(lo_ok[n_], 1)
                if shared(u) or routed(u):
                    wait(dve, hid_turned, u - 1)
                    wait(dve, silu_ok, u + 1)
                    dve.tensor_tensor(hid[u.odd][:, 0:INTER], silu[:], ps_h3[:, 0:INTER], ALU.mult).then_inc(hid_ok, 1)
                v = u - 1
                if shared(v) or routed(v):
                    wait(dve, hTh_ok, v + 1)
                    dve.tensor_tensor(hT_lo[v.odd][:], ps_ht[:, 0:IPAD], hT_hi[v.odd][:].bitcast(F32),
                                      ALU.subtract).then_inc(hTl_ok, 1)
                for j in turned_at(u):
                    tile_lo(j)
                if u.within(3, UNITS2 + 2) and u.odd:
                    j = (u - 3).half()
                    wait(dve, x2_in[j.odd], (j.half() + 1) * 16)
                    wait(dve, out_ok[j.odd], j.half() * 16)
                    wait(dve, down_ok, (j + 1) * 2)
                    dve.scalar_tensor_tensor(ys[j.odd][:], ps_y[:], small[:, 2:3], x2in[j.odd][:],
                                             ALU.mult, ALU.add).then_inc(y_ok, 1)

            count = [0]

            def did(ins):
                count[0] += 1
                ins.then_inc(rt, 1)

            def chain():
                dve.wait_ge(rt, count[0])

            def b3(t_, dims):
                return view(t_, 0, dims)

            E_, T_ = EXPERTS, TILES

            def pick_experts(tiles):
                for t in tiles:
                    did(dve.max(mx[:, t, :], logits[:, t * E_:(t + 1) * E_]))
                chain()
                for t in tiles:
                    did(dve.max_index(mi[:, t, :], mx[:, t, :], logits[:, t * E_:(t + 1) * E_]))

            def masks():
                chain()
                assert count[0] == R_PICK
                for k in range(2):
                    did(dve.tensor_copy(pick[:, k, :], mi[:, :, k]))
                chain()
                for k in range(2):
                    did(dve.tensor_tensor(mask[k][:], view(io[:], 0, [[0, T_], [1, E_]]),
                                          view(pick[:, k, :], 0, [[1, T_], [0, E_]]), ALU.is_equal))
                did(dve.tensor_tensor(lex[:, :, 0:E_], logits[:].rearrange("p (t e) -> p t e", e=E_),
                                      view(mx[:], 0, [[8, T_], [0, E_]]), ALU.subtract))
                did(dve.tensor_tensor(lex[:, :, E_:E_ + 1], mx[:, :, 1:2], mx[:, :, 0:1], ALU.subtract))
                chain()
                did(dve.tensor_tensor(both[:], mask[0][:], mask[1][:], ALU.add))
                assert count[0] == R_EXP
                dve.wait_ge(rt, count[0])
                dve.tensor_copy(hop[:, 1:2], hop[:, 0:1]).then_inc(r_both, 1)

            def softmax_weights():
                dve.wait_ge(r_exp, 1)
                did(dve.tensor_reduce(ssum[:], lex[:, :, 0:E_], AX.X, ALU.add))
                chain()
                did(dve.reciprocal(ssum[:], ssum[:]))
                chain()
                did(dve.tensor_scalar(wts[:, 0, :], ssum[:], small[:, 2:3], None, ALU.mult))
                chain()
                did(dve.tensor_tensor(wts[:, 1, :], lex[:, :, E_], wts[:, 0, :], ALU.mult))
                chain()
                flat = wts[:].rearrange("p k t -> p (k t)")
                did(dve.tensor_copy(wpart[:, 0, :], flat))
                chain()
                did(dve.tensor_tensor(wres[:], flat, wpart[:, 0, :], ALU.subtract))
                chain()
                did(dve.tensor_copy(wpart[:, 1, :], wres[:]))
                chain()
                did(dve.tensor_tensor(wres[:], wres[:], wpart[:, 1, :], ALU.subtract))
                chain()
                did(dve.tensor_copy(wpart[:, 2, :], wres[:]))

            def tile_bases():
                dve.wait_ge(r_count, 1)
                chain()
                did(dve.tensor_copy(cum[0][:], ps_total[:, 0:T_ * E_].rearrange("p (t e) -> p t e", e=E_)))
                a = 0
                d = 1
                while d < T_:
                    chain()
                    did(dve.tensor_copy(cum[1 - a][:, 0:d, :], cum[a][:, 0:d, :]))
                    did(dve.tensor_tensor(cum[1 - a][:, d:, :], cum[a][:, d:, :], cum[a][:, 0:T_ - d, :], ALU.add))
                    a, d = 1 - a, 2 * d
                chain()
                did(dve.tensor_tensor(cmp[:], view(cum[a][:, T_ - 1, :], 0, [[1, E_], [0, T_]]),
                                      view(tcmp[:], 0, [[0, E_], [1, T_]]), ALU.is_gt))
                chain()
                did(dve.tensor_reduce(ntile0[:], cmp[:], AX.X, ALU.add))
                chain()
                did(dve.tensor_copy(ntile[0][:], ntile0[:]))
                b, d = 0, 1
                while d < E_:
                    chain()
                    did(dve.tensor_copy(ntile[1 - b][:, 0:d], ntile[b][:, 0:d]))
                    did(dve.tensor_tensor(ntile[1 - b][:, d:], ntile[b][:, d:], ntile[b][:, 0:E_ - d], ALU.add))
                    b, d = 1 - b, 2 * d
                chain()
                did(dve.tensor_tensor(ntile[1 - b][:], ntile[b][:], ntile0[:], ALU.subtract))
                chain()
                did(dve.tensor_scalar(ntile[1 - b][:], ntile[1 - b][:], float(P), None, ALU.mult))
                chain()
                o = cum[1 - a]
                did(dve.tensor_copy(o[:, 0, :], ntile[1 - b][:]))
                did(dve.tensor_tensor(o[:, 1:, :], cum[a][:, 0:T_ - 1, :],
                                      view(ntile[1 - b][:], 0, [[0, T_ - 1], [1, E_]]), ALU.add))
                chain()
                did(dve.tensor_tensor(cum[a][:], ps_rank[:, 0:T_ * E_].rearrange("p (t e) -> p t e", e=E_), o[:], ALU.add))
                for k in range(2):
                    chain()
                    did(dve.tensor_tensor(mask[k][:], mask[k][:], cum[a][:], ALU.mult))
                chain()
                for k in range(2):
                    did(dve.tensor_reduce(slot[:, k * T_:(k + 1) * T_], mask[k][:], AX.X, ALU.add))
                chain()
                did(dve.tensor_copy(sloti[:, 0, :], slot[:]))
                chain()
                did(dve.tensor_scalar(sloti[:, 1, :], sloti[:, 0, :], 7, None, ALU.logical_shift_right))
                did(dve.tensor_scalar(sloti[:, 2, :], sloti[:, 0, :], P - 1, None, ALU.bitwise_and))
                chain()
                did(dve.tensor_copy(slotb[:], sloti[:, 1:3, :]))
                did(dve.tensor_tensor(tcmp[:], view(ntile[b][:], 0, [[0, SLOTS], [1, E_]]),
                                      view(io[:], 0, [[1, SLOTS], [0, E_]]), ALU.is_le))
                chain()
                did(dve.tensor_reduce(texp[:, 1:], tcmp[:], AX.X, ALU.add))
                chain()
                did(dve.tensor_scalar(texp[:, 1:], texp[:, 1:], float(E_ - 1), float(P), ALU.min, ALU.mult))
                chain()
                did(dve.tensor_tensor(tmpf[:], texp[:, 1:], texp[:, 0:SLOTS], ALU.not_equal))
                ti = tile_info[:].rearrange("p (s k) -> p s k", k=2)
                did(dve.tensor_copy(ti[:, :, 0], texp[:, 1:]))
                chain()
                did(dve.tensor_copy(ti[:, :, 1], tmpf[:]))

            NK = 2 * T_

            def spread(part):
                chain()
                if part < 4:
                    n0 = part * NK // 4
                    did(dve.tensor_tensor(place[:, n0:n0 + NK // 4, :], view(iob[:], 0, [[0, NK // 4], [1, P]]),
                                          view(slotb[:, 1, :], n0, [[1, NK // 4], [0, P]]), ALU.is_equal))
                    return
                f = field
                row = FIELDS * SLOTS

                def fv(n_):
                    return view(f[:], n_ * SLOTS, [[row, NK], [1, SLOTS]])
                if part == 4:
                    did(dve.tensor_tensor(fv(2), view(iob[:], 0, [[0, NK], [1, SLOTS]]),
                                          view(slotb[:, 0, :], 0, [[1, NK], [0, SLOTS]]), ALU.is_equal))
                    chain()
                    did(dve.tensor_tensor(fv(0), fv(2), view(trow[:], 0, [[1, NK], [0, SLOTS]]), ALU.mult))
                    did(dve.tensor_tensor(fv(1), fv(2), view(prow[:], 0, [[1, NK], [0, SLOTS]]), ALU.mult))
                if part == 5:
                    for n_ in range(3):
                        did(dve.tensor_tensor(fv(3 + n_), fv(2), view(wpart[:, n_, :], 0, [[1, NK], [0, SLOTS]]), ALU.mult))
                    chain()
                    dve.tensor_copy(hop[:, 1:2], hop[:, 0:1]).then_inc(r_fields, 1)

            def tables():
                dve.wait_ge(r_table, 1)
                chain()
                did(dve.tensor_copy(tab[:], ps_table[:, 0:FIELDS * SLOTS].rearrange("p (f s) -> p f s", s=SLOTS)))
                chain()
                si = slot_info[:].rearrange("p (s k) -> p s k", k=3)
                sf = slot_info[:].bitcast(F32).rearrange("p (s k) -> p s k", k=3)
                did(dve.scalar_tensor_tensor(tab[:, 0, :], tab[:, 0, :], float(P), tab[:, 1, :], ALU.mult, ALU.add))
                did(dve.tensor_scalar(tab[:, 2, :], tab[:, 2, :], -float(SKIP), float(SKIP), ALU.mult, ALU.add))
                did(dve.tensor_tensor(tab[:, 4, :], tab[:, 4, :], tab[:, 5, :], ALU.add))
                chain()
                did(dve.tensor_copy(si[:, :, 0], tab[:, 0, :]))
                did(dve.tensor_tensor(tab[:, 2, :], tab[:, 2, :], tab[:, 0, :], ALU.add))
                did(dve.tensor_tensor(sf[:, :, 2], tab[:, 3, :], tab[:, 4, :], ALU.add))
                chain()
                did(dve.tensor_copy(si[:, :, 1], tab[:, 2, :]))
                chain()
                dve.tensor_copy(hop[:, 1:2], hop[:, 0:1]).then_inc(r_done, 1)

            def after(u):
                if u == -1:
                    logits_copy(At(TILES - 1))
                    dve.wait_ge(logits_ok, TILES)
                    dve.wait_ge(r_const, 1)
                    dve.memset(texp[:, 0:1], -1.0).then_inc(rt, 1)
                    count[0] += 1
                    did(dve.tensor_scalar(tcmp[:, 0, 0:T_], io[:, 0:T_], float(P), None, ALU.mult))
                if u == 0:
                    pick_experts(range(T_))
                if u == 1:
                    masks()
                if u == 5:
                    softmax_weights()
                if u == 6:
                    tile_bases()
                if 7 <= u < 13:
                    spread(u - 7)
                if u == 14:
                    tables()

            steps(dve, step, after)

        @block.tensor
        def _(pe):
            pe.wait_ge(setup_pool, 2)

            def turn_rows(src, dst, ok):
                for c in range(BLOCKS):
                    last = pe.transpose(dst[:, c * P:(c + 1) * P], src[:, c * P:(c + 1) * P], ident[:])
                last.then_inc(ok, 1)

            def turn_q(t):
                wait(pe, q_ok, t * 2)
                wait(pe, xn_ok, t + 1)
                turn_rows(xn[t.odd], ps_q, q_turned)

            def turn_t(t):
                wait(pe, tT_ok, t)
                wait(pe, t_ok, t + 1)
                turn_rows(tn[t.odd], ps_t, t_turned)

            def gate(t):
                wait(pe, logits_ok, t)
                wait(pe, tT_ok, t + 1)
                for c in range(BLOCKS):
                    last = pe.matmul(ps_gate[:, 0:EXPERTS], tT[:, c * P:(c + 1) * P],
                                     gw[:, c * EXPERTS:(c + 1) * EXPERTS], start=(c == 0), stop=(c == BLOCKS - 1))
                last.then_inc(gate_ok, 1)

            def conv(t, lb):
                p = t.odd
                n = BATCH * PAIRS
                for h in range(2):
                    if h == 0:
                        if lb == 0:
                            wait(pe, toep_in[p], (t.half() + 1) * 16)
                            wait(pe, kv_ok, (t + 1) * 2)
                        wait(pe, prod_ok, (t * 4 + lb - 1) * 6)
                    for mb in range(lb + 1):
                        d = lb - mb
                        o = (mb * 2 + h) * n
                        mm = pe.matmul(ps_conv[lb % 2][h][:, 0:n], toep[p][:, h * L + d * P:h * L + (d + 1) * P],
                                       kv[p][:, o:o + n], start=(mb == 0), stop=(mb == lb))
                    mm.then_inc(conv_ok, 1)

            def sum_rows(t, lb):
                if lb == 0:
                    wait(pe, x2_ok, t)
                wait(pe, prod_ok, (t * 4 + lb + 1) * 6)
                for r in range(SUMROWS):
                    mm = pe.matmul(ps_o[:, lb * P:(lb + 1) * P],
                                   prod[lb % 2][:, r * P:(r + 1) * P], ident[:],
                                   is_transpose=True, start=(r == 0), stop=(r == SUMROWS - 1))
                mm.then_inc(summed, 1)

            turn_q(At(0))

            def turn(t):
                first, last = t.within(0, 1), t.within(TILES - 1, TILES)
                conv(t, 0)
                if not first:
                    sum_rows(t - 1, 3)
                conv(t, 1)
                sum_rows(t, 0)
                conv(t, 2)
                sum_rows(t, 1)
                if not first:
                    turn_t(t - 1)
                if not last:
                    turn_q(t + 1)
                conv(t, 3)
                if not first:
                    gate(t - 1)
                sum_rows(t, 2)

            pairs(pe, turn)
            sum_rows(At(TILES - 1), 3)
            turn_t(At(TILES - 1))
            gate(At(TILES - 1))

            def turn_tile(j):
                if j.within(0, TILES):
                    wait(pe, tn_in[j.odd], (j.half() + 1) * 16)
                else:
                    wait(pe, row_in[j.odd], ((j - TILES).half() + 1) * 16)
                wait(pe, tTl_ok, j)
                if j.within(0, 1):
                    wait(pe, tT_ok, TILES)
                turn_rows(tn[j.odd], ps_t, tile_turned)

            def parts(hi, lo, whi, wlo):
                return (hi, whi), (hi, wlo), (lo, whi)

            def up(u):
                j = tile_of(u)
                wait(pe, hid_ok, u)
                if shared(u):
                    whi, wlo, o = shared_hi, shared_lo, u.odd * WROW
                    wait(pe, slo_ok, TILES)
                else:
                    whi, wlo, o = w_hi[u.odd], w_lo[u.odd], 0
                    wait(pe, lo_ok[0], u - UNITS2 + 1)
                    wait(pe, lo_ok[1], u - UNITS2 + 1)
                wait(pe, tTl_ok, j + 1)
                for c in range(BLOCKS):
                    for k, (a, w) in enumerate(parts(tT_hi[j.odd], tT_lo[j.odd], whi, wlo)):
                        for n_, dst in enumerate((ps_h1, ps_h3)):
                            f = o + (c * 2 + n_) * INTER
                            mm = pe.matmul(dst[:, 0:INTER], a[:, c * P:(c + 1) * P], w[:, f:f + INTER],
                                           start=(c == 0 and k == 0), stop=(c == BLOCKS - 1 and k == 2))
                mm.then_inc(up_ok, 1)

            def turn_hidden(u):
                wait(pe, hTl_ok, u)
                wait(pe, hid_ok, u + 1)
                for c in range(ICH):
                    last = pe.transpose(ps_ht[:, c * P:(c + 1) * P], hid[u.odd][:, c * P:(c + 1) * P], ident[:])
                last.then_inc(hid_turned, 1)

            def down(u):
                if shared(u):
                    whi, wlo, o = shared_hi, shared_lo, u.odd * WROW + W13
                    if not u.odd:
                        wait(pe, y_ok, u.half())
                    first, last = not u.odd, bool(u.odd)
                else:
                    whi, wlo, o = w_hi[u.odd], w_lo[u.odd], W13
                    if u.within(UNITS2, UNITS2 + 1):
                        wait(pe, y_ok, TILES)
                    wait(pe, yr_ok, u - UNITS2)
                    wait(pe, hi_ok[2], u - UNITS2 + 1)
                    wait(pe, lo_ok[2], u - UNITS2 + 1)
                    first = last = True
                wait(pe, hTl_ok, u + 1)
                for c in range(ICH):
                    for k, (a, w) in enumerate(parts(hT_hi[u.odd], hT_lo[u.odd], whi, wlo)):
                        mm = pe.matmul(ps_y[:], a[:, c * P:(c + 1) * P], w[:, o + c * L:o + (c + 1) * L],
                                       start=(first and c == 0 and k == 0), stop=(last and c == ICH - 1 and k == 2))
                mm.then_inc(down_ok, 1)

            def step(u):
                if shared(u) or routed(u):
                    up(u)
                if shared(u - 1) or routed(u - 1):
                    turn_hidden(u - 1)
                for j in turned_at(u):
                    turn_tile(j)
                if shared(u - 2) or routed(u - 2):
                    down(u - 2)

            def after(u):
                if u == 3:
                    pe.wait_ge(r_both, 1)
                    pe.wait_ge(x2_ok, TILES)
                    pe.wait_ge(q_ok, 2 * TILES)
                    n = TILES * EXPERTS
                    flat = both[:].rearrange("p t e -> p (t e)")
                    pe.matmul(ps_rank[:, 0:n], upper[:], flat, start=True, stop=True)
                    pe.matmul(ps_total[:, 0:n], ones[:], flat, start=True, stop=True).then_inc(r_count, 1)
                if u == 14:
                    pe.wait_ge(r_fields, 1)
                    for k in range(2 * TILES):
                        mm = pe.matmul(ps_table[:, 0:FIELDS * SLOTS], place[:, k, :],
                                       field[:, k, :, :].rearrange("p f s -> p (f s)"),
                                       start=(k == 0), stop=(k == 2 * TILES - 1))
                    mm.then_inc(r_table, 1)

            steps(pe, step, after)

        @block.gpsimd
        def _(pool):
            pool.iota(ys[0][:, 0:P], [[1, P]], base=0, channel_multiplier=-1,
                      allow_small_or_imprecise_dtypes=True).then_inc(setup_pool, 1)
            pool.wait_ge(setup_pool, 1)
            pool.tensor_scalar(ident[:], ys[0][:, 0:P], 0.0, None, ALU.is_equal).then_inc(setup_pool, 1)

            def form(t):
                p = t.odd
                wait(pool, conv_ok, (t - 1) * 8)
                wait(pool, ctx_in[p], (t.half() + 1) * 16)
                g, hb = BLOCKS * 2, HD * BATCH
                pool.tensor_tensor(view(kv[p][:], 0, [[PAIRS * BATCH, g], [hb, 4], [1, hb]]),
                                   view(cx[p][:], 0, [[EXT * BATCH, g], [0, 4], [1, hb]]),
                                   view(cx[p][:], 0, [[EXT * BATCH, g], [BATCH, 4], [1, hb]]),
                                   ALU.mult).then_inc(kv_ok, 1)
                pool.tensor_tensor(view(kv[p][:], 4 * hb, [[PAIRS * BATCH, g], [1, hb // 2]]),
                                   view(cx[p][:], 0, [[EXT * BATCH, g], [1, hb // 2]]),
                                   view(cx[p][:], hb // 2, [[EXT * BATCH, g], [1, hb // 2]]),
                                   ALU.mult).then_inc(kv_ok, 1)

            def split_shared(t):
                p = t.odd
                o = t * STAGE
                wait(pool, shi_ok, t + 1)
                pool.tensor_tensor(shared_lo[:, bass.ds(o.v, STAGE)], raw[:, p * STAGE:(p + 1) * STAGE],
                                   shared_hi[:, bass.ds(o.v, STAGE)].bitcast(F32), ALU.subtract).then_inc(slo_ok, 1)

            form(At(0))

            def turn(t):
                if not t.within(TILES - 1, TILES):
                    form(t + 1)
                split_shared(t)

            pairs(pool, turn)
            pool.wait_ge(conv_ok, 8 * TILES)
            pool.wait_ge(summed, 4 * TILES)
            pool.wait_ge(gate_ok, TILES)
            pool.wait_ge(t_ok, TILES)
            for p in (0, 1):
                pool.wait_ge(x2_out[p], 16 * TILES // 2)
            pool.iota(io[:], [[1, P]], base=0, channel_multiplier=0,
                      allow_small_or_imprecise_dtypes=True).then_inc(setup_pool, 1)
            pool.iota(place[:, 0, :], [[1, P]], base=0, channel_multiplier=-1,
                      allow_small_or_imprecise_dtypes=True).then_inc(setup_pool, 1)
            pool.iota(pid[:], [[0, 1]], base=0, channel_multiplier=1,
                      allow_small_or_imprecise_dtypes=True).then_inc(setup_pool, 1)
            pool.iota(trow[:], [[0, 2], [1, TILES]], base=0, channel_multiplier=0,
                      allow_small_or_imprecise_dtypes=True).then_inc(setup_pool, 1)
            pool.iota(prow[:], [[0, 2 * TILES]], base=0, channel_multiplier=1,
                      allow_small_or_imprecise_dtypes=True).then_inc(setup_pool, 1)
            pool.memset(ones[:], 1.0).then_inc(setup_pool, 1)
            pool.memset(phop[:], 0.0).then_inc(setup_pool, 1)
            pool.wait_ge(setup_pool, 9)
            pool.tensor_copy(iob[:], io[:]).then_inc(setup_pool, 1)
            pool.tensor_scalar(upper[:], place[:, 0, :], 0.0, None, ALU.is_gt).then_inc(setup_pool, 1)
            pool.wait_ge(setup_pool, 11)
            pool.tensor_copy(pid[:], pid[:]).then_inc(r_const, 1)

            def hold(n):
                pool.tensor_tensor(phop[:, n:n + 1], phop[:, 0:1], phop[:, 0:1], ALU.add)

            def gather(s):
                p = s.odd
                wait(pool, tile_turned, s + TILES - 1)
                wait(pool, row_in[p], s.half() * 16)
                pool.tensor_copy(gat_i[p][:], slot_info[:, bass.ds(s.v * 3, 3)]).then_inc(gidx_ok, 1)
                wait(pool, gidx_ok, s + 1)
                hold(1 + p)
                pool.indirect_dma_start(out=tn[p][:], out_offset=None, in_=t_rows,
                                        in_offset=bass.IndirectOffsetOnAxis(ap=gat_i[p][:, 0:1], axis=0),
                                        bounds_check=ROWS - 1, oob_is_err=False).then_inc(row_in[p], 16)

            def scatter(s):
                p = s.odd
                if s.within(0, 1):
                    for k in (0, 1):
                        pool.wait_ge(out_ok[k], 16 * TILES // 2)
                wait(pool, yr_ok, s + 1)
                prev = s - 1
                if not s.within(0, 1):
                    wait(pool, added[prev.odd], (prev.half() + 1) * 16)
                hold(3 + p)
                pool.indirect_dma_start(out=out, out_offset=bass.IndirectOffsetOnAxis(ap=sca_i[p][:, 1:2], axis=0),
                                        in_=ys[p][:], in_offset=None, bounds_check=ROWS - 1, oob_is_err=False,
                                        compute_op=ALU.add).then_inc(added[p], 16)

            def scatter_index(s):
                p = s.odd
                wait(pool, added[p], s.half() * 16)
                pool.tensor_copy(sca_i[p][:], slot_info[:, bass.ds(s.v * 3, 3)]).then_inc(sidx_ok, 1)

            def step(u):
                s = u - UNITS2
                if routed(u + 3):
                    if s.within(-3, -2):
                        pool.wait_ge(r_done, 1)
                    gather(s + 3)
                if routed(u - 1):
                    v = u - 1
                    a, b = PIECE[2]
                    wait(pool, hi_ok[2], v - UNITS2 + 1)
                    pool.tensor_tensor(w_lo[v.odd][:, a:b], raw[:, a:b], w_hi[v.odd][:, a:b].bitcast(F32),
                                       ALU.subtract).then_inc(lo_ok[2], 1)
                if routed(u - 3):
                    scatter(s - 3)
                if routed(u - 2):
                    scatter_index(s - 2)

            steps(pool, step)


def kernel(**inputs):
    import numpy as np
    import concourse.bacc as bacc
    from concourse.bass_utils import run_bass_kernel_spmd as run

    def a(name):
        return np.asarray(inputs[name])

    x, c = a("x"), a("ctx_2048")
    x_rows = x.reshape(BATCH, TILES, 2, HD, L).transpose(1, 3, 2, 0, 4).reshape(ROWS, L)
    cc = c.reshape(BATCH, TILES, 2, HD, BLOCKS, P)[..., ::-1].transpose(1, 5, 4, 2, 3, 0)
    cc = np.concatenate([cc, cc[..., :EXT - HD, :]], axis=-2).reshape(TILES, P, BLOCKS * GROUPS * EXT)

    def up(w1, w3):
        w = np.stack([w1, w3], 1).reshape(-1, 2, INTER, BLOCKS, P)
        return w.transpose(0, 4, 3, 1, 2).reshape(-1, P, W13)

    def down(w2):
        w = np.zeros((w2.shape[0], IPAD, L), w2.dtype)
        w[:, :INTER] = w2.transpose(0, 2, 1)
        return w.reshape(-1, ICH, P, L).transpose(0, 2, 1, 3).reshape(-1, P, W2)

    sw1, sw3 = (a("L0_ffn_" + n).reshape(SHARED, INTER, L) for n in ("sw1", "sw3"))
    sw2 = a("L0_ffn_sw2").reshape(L, SHARED, INTER).transpose(1, 0, 2)
    routed = np.concatenate([up(a("L0_ffn_w1"), a("L0_ffn_w3")), down(a("L0_ffn_w2"))], 2)
    shared = np.concatenate([up(sw1, sw3), down(sw2)], 2)
    shared = shared.transpose(1, 0, 2).reshape(P, TILES, STAGE).transpose(1, 0, 2).reshape(SHARED * P, WROW)
    weights = np.concatenate([routed.reshape(EXPERTS * P, WROW), shared], 0)
    arrays = {
        "in_x": x_rows,
        "in_ctx": cc,
        "in_conv": a("L0_xattn_ssm_kernel"),
        "in_d": a("L0_xattn_D").reshape(HEADS, 1),
        "in_gates": np.broadcast_to(np.concatenate([a("g_xattn"), a("g_ffn")])[None], (P, 2)),
        "in_gate_w": a("L0_ffn_gate_w").T.reshape(BLOCKS, P, EXPERTS).transpose(1, 0, 2).reshape(P, BLOCKS * EXPERTS),
        "in_weights": weights,
    }
    arrays = {k: np.ascontiguousarray(v) for k, v in arrays.items()}
    nc = bacc.Bacc("TRN2", target_bir_lowering=False, num_devices=1)
    aps = [nc.dram_tensor(k, v.shape, mybir.dt.from_np(v.dtype), kind="ExternalInput").ap() for k, v in arrays.items()]
    aps.append(nc.dram_tensor("out_0", (ROWS, L), F32, kind="ExternalOutput").ap())
    program(nc, *aps)
    got = run(nc, [arrays], core_ids=[0]).results[0]["out_0"]
    return got.reshape(TILES, HD, 2, BATCH, L).transpose(3, 0, 2, 1, 4).reshape(BATCH, HEADS * HD, L)
```

```python
from contextlib import ExitStack

import concourse.bass as bass
from concourse import mybir

F32 = mybir.dt.float32
F32R = mybir.dt.float32r
BF16 = mybir.dt.bfloat16
I32 = mybir.dt.int32
U32 = mybir.dt.uint32
ALU = mybir.AluOpType
ACT = mybir.ActivationFunctionType
AX = mybir.AxisListType

P = 128
BATCH, HEADS, HD, L = 8, 32, 8, 512
ROWS = BATCH * HEADS * HD
TILES = ROWS // P
BLOCKS = L // P
PAIRS = HD * (HD + 1) // 2
EXT = HD + HD // 2
GROUPS = 2 * BATCH
SUMROWS = 9
EXPERTS, INTER = 16, 352
SHARED = 2
W13 = BLOCKS * 2 * INTER
ICH = (INTER + P - 1) // P
IPAD = ICH * P
W2 = ICH * L
WROW = W13 + W2
HALF = W13 // 2
UNITS2 = SHARED * TILES
SLOT_TILES = (2 * ROWS + EXPERTS * (P - 1)) // P
SLOTS = SLOT_TILES + 1
KV_DVE = 1536
STAGE = SHARED * WROW // TILES
EPS = 1e-5
SKIP = 1 << 20
INFO = 6
FIELDS = 6


class At:

    def __init__(self, b, a=0, i=None, n=1):
        self.a, self.b, self.i, self.n = (a, b, i, n) if i is not None else (0, b, None, 1)

    def __add__(self, k):
        return At(self.b + k, self.a, self.i, self.n)

    def __sub__(self, k):
        return self + (-k)

    def __mul__(self, k):
        return At(self.b * k, self.a * k, self.i, self.n)

    def half(self):
        assert self.a % 2 == 0
        return At(self.b // 2, self.a // 2, self.i, self.n)

    @property
    def odd(self):
        assert self.a % 2 == 0
        return self.b % 2

    def within(self, low, high):
        ends = {low <= self.b < high, low <= self.b + self.a * (self.n - 1) < high}
        assert len(ends) == 1
        return ends.pop()

    @property
    def v(self):
        return self.b if self.i is None else self.i * self.a + self.b


def wait(eng, sem, count):
    count = count if isinstance(count, At) else At(count)
    if count.i is None and count.b <= 0:
        return
    assert count.b > 0
    eng.wait_ge(sem, count.v)


def view(ap, offset, dims):
    return bass.AP(ap.tensor, ap.offset + offset, [list(ap.ap[0])] + dims)


def program(nc, x, ctx_ext, conv_rows, conv_d, gates, gate_w, weights, out):
    ctx = ExitStack()
    with ctx:
        def sem(name):
            return ctx.enter_context(nc.semaphore(name))

        def sem2(name):
            return [sem(name + "0"), sem(name + "1")]

        def sb(name, shape, dt=F32, stack=ctx):
            return stack.enter_context(nc.sbuf_tensor(name, shape, dt))

        def sb2(name, shape, dt=F32, stack=ctx):
            return [sb(name + "0", shape, dt, stack), sb(name + "1", shape, dt, stack)]

        kpad = nc.dram_tensor("kpad", (HEADS, 640), F32, kind="Internal").ap()
        x2_rows = nc.dram_tensor("x2_rows", (ROWS, L), F32, kind="Internal").ap()
        t_rows = nc.dram_tensor("t_rows", (ROWS, L), F32, kind="Internal").ap()
        tT_rows = nc.dram_tensor("tT_rows", (ROWS, L), F32, kind="Internal").ap()
        toeplitz = bass.AP(kpad.tensor, 0, [[2 * 640, TILES], [1, P], [640, 2], [1, L]])
        x_t = x.rearrange("(t p) l -> t p l", p=P)
        x2_t = x2_rows.rearrange("(t p) l -> t p l", p=P)
        t_t = t_rows.rearrange("(t p) l -> t p l", p=P)
        tT_t = tT_rows.rearrange("(t p) l -> t p l", p=P)
        out_t = out.rearrange("(t p) l -> t p l", p=P)

        bank = [ctx.enter_context(nc.psum_tensor(f"bank{n}", [P, 512], F32)) for n in range(8)]
        ps_conv = [[bank[0], bank[1]], [bank[2], bank[3]]]
        ps_o, ps_q, ps_t, ps_gate = bank[4], bank[5], bank[6], bank[7]
        ps_h1, ps_h3, ps_ht, ps_y = bank[0], bank[1], bank[2], bank[3]
        ps_rank, ps_total, ps_table = bank[4], bank[5], bank[7]

        ident = sb("ident", [P, P])
        small = sb("small", [P, 8])
        gts = sb("gts", [P, 2])
        ahop = sb("ahop", [P, 5])
        hop, phop = sb("hop", [P, 2]), sb("phop", [P, 5])
        gw = sb("gw", [P, BLOCKS * EXPERTS])
        shared_hi = sb("shared_hi", [P, SHARED * WROW], F32R)
        shared_lo = sb("shared_lo", [P, SHARED * WROW], F32R)
        logits = sb("logits", [P, TILES * EXPERTS])
        slot_info = sb("slot_info", [P, 3 * SLOTS], I32)
        tile_info = sb("tile_info", [P, INFO * SLOTS], I32)
        gat_i = sb2("gat_i", [P, 3], I32)
        sca_i = sb2("sca_i", [P, 3], I32)

        one = ExitStack()
        cx = sb2("cx", [P, BLOCKS * GROUPS * EXT], F32, one)
        toep = sb2("toep", [P, 2 * L], F32, one)
        stage = sb2("stage", [P, STAGE], F32, one)
        toep_hi, toep_lo = sb2("toep_hi", [P, 2 * L], F32R, one), sb2("toep_lo", [P, 2 * L], F32R, one)
        tT = sb2("tT", [P, L], F32, one)
        t1 = sb2("t1", [P, L], F32, one)
        x2 = sb2("x2", [P, L], F32, one)
        st1, st2 = sb2("st1_", [P, 6], F32, one), sb2("st2_", [P, 6], F32, one)
        mv1, mv2 = sb2("mv1_", [P, 2], F32, one), sb2("mv2_", [P, 2], F32, one)
        sd1, sd2 = sb2("sd1_", [P, 2], F32, one), sb2("sd2_", [P, 2], F32, one)
        kv = sb("kv", [P, BLOCKS * GROUPS * PAIRS], F32, one)
        kv_hi = sb2("kv_hi", [P, BLOCKS * GROUPS * PAIRS], F32R, one)
        kv_lo = sb2("kv_lo", [P, BLOCKS * GROUPS * PAIRS], F32R, one)
        xt = sb2("xt", [P, L], F32, one)
        xr = sb2("xr", [P, L], F32, one)
        xn = sb2("xn", [P, L], F32, one)
        q = sb2("q", [P, BLOCKS * GROUPS * EXT], F32, one)
        prod = sb2("prod", [P, SUMROWS * P], F32, one)
        krow = sb("krow", [HEADS, 640], F32, one)
        drow = sb("drow", [HEADS, 1], F32, one)
        one.close()
        tn = sb2("tn", [P, L])
        x2in = sb2("x2in", [P, L])
        tT_hi = sb2("tT_hi", [P, L], F32R)
        tT_lo = sb2("tT_lo", [P, L], F32R)
        silu = sb("silu", [P, INTER])
        hid = sb2("hid", [P, IPAD])
        hT_hi = sb2("hT_hi", [P, IPAD], F32R)
        hT_lo = sb2("hT_lo", [P, IPAD], F32R)
        ys = sb2("ys", [P, L])
        w_hi = [sb("w_hi0", [P, WROW], F32R)]
        w_lo = [sb("w_lo0", [P, WROW], F32R)]
        route = ExitStack()
        io = sb("io", [P, P], F32, route)
        iob = sb("iob", [P, P], BF16, route)
        upper = sb("upper", [P, P], BF16, route)
        ones = sb("ones", [P, P], BF16, route)
        mx = sb("mx", [P, TILES, 8], F32, route)
        mi = sb("mi", [P, TILES, 8], U32, route)
        pick = sb("pick", [P, 2, TILES], F32, route)
        mask = [sb(f"mask{k}", [P, TILES, EXPERTS], F32, route) for k in range(2)]
        both = sb("both", [P, TILES, EXPERTS], BF16, route)
        lex = sb("lex", [P, TILES, EXPERTS + 1], F32, route)
        ssum = sb("ssum", [P, TILES], F32, route)
        wts = sb("wts", [P, 2, TILES], F32, route)
        wres = sb("wres", [P, 2 * TILES], F32, route)
        wpart = sb("wpart", [P, 3, 2 * TILES], BF16, route)
        cum = sb2("cum", [P, TILES, EXPERTS], F32, route)
        cmp = sb("cmp", [P, EXPERTS, TILES], F32, route)
        ntile = sb2("ntile", [P, EXPERTS], F32, route)
        ntile_own = sb("ntile_own", [P, EXPERTS], F32, route)
        slot = sb("slot", [P, 2 * TILES], F32, route)
        sloti = sb("sloti", [P, 3, 2 * TILES], I32, route)
        slotb = sb("slotb", [P, 2, 2 * TILES], BF16, route)
        prow = sb("prow", [P, 2 * TILES], BF16, route)
        trow = sb("trow", [P, 2 * TILES], BF16, route)
        place = sb("place", [P, 2 * TILES, P], BF16, route)
        field = sb("field", [P, 2 * TILES, FIELDS, SLOTS], BF16, route)
        tab = sb("tab", [P, FIELDS, SLOTS], F32, route)
        tcmp = sb("tcmp", [P, SLOTS, EXPERTS], F32, route)
        texp = sb("texp", [P, SLOTS + 1], F32, route)
        tmpf = sb("tmpf", [P, SLOTS], F32, route)
        tnum = sb("tnum", [P, SLOTS], F32, route)
        inum = sb("inum", [P, SLOTS], I32, route)
        pid = sb("pid", [P, 1], F32, route)
        route.close()
        w_hi.append(sb("w_hi1", [P, WROW], F32R))
        w_lo.append(sb("w_lo1", [P, WROW], F32R))
        raw_up = sb("raw_up", [P, 2 * W13])
        raw_down = sb("raw_down", [P, W2])

        consts_in, kpad_in, kpad_ok, kpad_out = sem("consts_in"), sem("kpad_in"), sem("kpad_ok"), sem("kpad_out")
        setup_dve, setup_pool, gate_tanh = sem("setup_dve"), sem("setup_pool"), sem("gate_tanh")
        x_in, xr_in, ctx_in, toep_in, stage_in = (sem2(n) for n in ("x_in", "xr_in", "ctx_in", "toep_in", "stage_in"))
        stat1, std1, rstd1, xn_ok = sem("stat1"), sem("std1"), sem("rstd1"), sem("xn_ok")
        q_turned, q_ok, kv_ok = sem("q_turned"), sem("q_ok"), sem("kv_ok")
        kvh_ok, kvl_ok, kvl2_ok = sem("kvh_ok"), sem("kvl_ok"), sem("kvl2_ok")
        toeph_ok, toepl_ok = sem("toeph_ok"), sem("toepl_ok")
        conv_ok, prod_ok, summed = sem("conv_ok"), sem("prod_ok"), sem("summed")
        x2_ok, stat2, std2, rstd2, t_ok = sem("x2_ok"), sem("stat2"), sem("std2"), sem("rstd2"), sem("t_ok")
        t_turned, tT_ok, gate_ok, logits_ok = sem("t_turned"), sem("tT_ok"), sem("gate_ok"), sem("logits_ok")
        shi_ok, slo_ok = sem("shi_ok"), sem("slo_ok")
        x2_out, t_out, tT_out = sem2("x2_out"), sem2("t_out"), sem2("tT_out")
        rt, r_const, r_exp, r_count, r_table = sem("rt"), sem("r_const"), sem("r_exp"), sem("r_count"), sem("r_table")
        r_both, r_tiles, r_places, r_weights, r_fields, r_done = (sem(n) for n in ("r_both", "r_tiles", "r_places", "r_weights", "r_fields", "r_done"))
        tn_in, x2_in, row_in = sem2("tn_in"), sem2("x2_in"), sem2("row_in")
        tile_turned, tTh_ok, tTl_ok = sem("tile_turned"), sem("tTh_ok"), sem("tTl_ok")
        up_ok, silu_ok, hid_ok = sem("up_ok"), sem("silu_ok"), sem("hid_ok")
        hid_turned, hTh_ok, hTl_ok, down_ok = sem("hid_turned"), sem("hTh_ok"), sem("hTl_ok"), sem("down_ok")
        y_ok, yr_ok, out_ok = sem("y_ok"), sem("yr_ok"), sem2("out_ok")
        raw_in = [sem2("rawA_in"), sem2("rawB_in"), sem2("rawC_in")]
        hi_ok = [sem("hiA_ok"), sem("hiB_ok"), sem("hiC_ok")]
        lo_ok = [sem("loA_ok"), sem("loB_ok"), sem("loC_ok")]
        gidx_ok, sidx_ok, added, hid_zero = sem("gidx_ok"), sem("sidx_ok"), sem2("added"), sem("hid_zero")
        PIECE = [(0, HALF), (HALF, W13), (W13, WROW)]

        block = ctx.enter_context(nc.Block())

        def pairs(eng, turn):
            for t in range(3):
                turn(At(t))
            n = (TILES - 4) // 2
            with eng.Fori(0, n) as i:
                for o in (3, 4):
                    turn(At(o, 2, i, n))
            turn(At(TILES - 1))

        LOOP2 = (16, 3)
        LOOP3 = (6, 19)
        LAST = SLOT_TILES + 3

        def steps(eng, step, after=lambda u: None):
            for u in range(-1, LOOP2[0]):
                step(At(u))
                after(u)
            with eng.Fori(0, LOOP2[1]) as i:
                for o in range(4):
                    step(At(LOOP2[0] + o, 4, i, LOOP2[1]))
            for u in range(LOOP2[0] + 4 * LOOP2[1], UNITS2 + LOOP3[0]):
                step(At(u))
            with eng.Fori(0, LOOP3[1]) as i:
                for o in range(2):
                    step(At(UNITS2 + LOOP3[0] + o, 2, i, LOOP3[1]))
            for u in range(UNITS2 + LOOP3[0] + 2 * LOOP3[1], UNITS2 + LAST):
                step(At(u))

        def shared(u):
            return u.within(0, UNITS2)

        def routed(u):
            return u.within(UNITS2, UNITS2 + SLOT_TILES)

        def tile_of(u):
            return u.half() if shared(u) else u - TILES

        def half_of(eng, s):
            return eng.value_load(tile_info[0:1, bass.ds(s.v * INFO + 2, 1)], min_val=0, max_val=W13)

        def wait_up(eng, n, s):
            wait(eng, raw_in[n][(s - 1).odd], ((s + 1).half()) * 16 if not (s - 1).odd else (s.half() + 1) * 16)

        def form(eng, t):
            p = t.odd
            wait(eng, kvl_ok, t)
            wait(eng, kvl2_ok, t)
            wait(eng, ctx_in[p], (t.half() + 1) * 16)
            g, hb = BLOCKS * 2, HD * BATCH
            eng.tensor_tensor(view(kv[:], 0, [[PAIRS * BATCH, g], [hb, 4], [1, hb]]),
                              view(cx[p][:], 0, [[EXT * BATCH, g], [0, 4], [1, hb]]),
                              view(cx[p][:], 0, [[EXT * BATCH, g], [BATCH, 4], [1, hb]]),
                              ALU.mult).then_inc(kv_ok, 1)
            eng.tensor_tensor(view(kv[:], 4 * hb, [[PAIRS * BATCH, g], [1, hb // 2]]),
                              view(cx[p][:], 0, [[EXT * BATCH, g], [1, hb // 2]]),
                              view(cx[p][:], hb // 2, [[EXT * BATCH, g], [1, hb // 2]]),
                              ALU.mult).then_inc(kv_ok, 1)

        def turned_at(u):
            if shared(u) and not u.odd:
                return [u.half() + 1]
            if u.within(UNITS2 - 1, UNITS2):
                return [At(TILES + 1)]
            if routed(u) and routed(u + 2):
                return [tile_of(u + 2)]
            return []

        R_PICK = 2 + 2 * TILES
        R_EXP = R_PICK + 7

        NK = 2 * TILES

        def field_of(n_):
            return view(field[:], n_ * SLOTS, [[FIELDS * SLOTS, NK], [1, SLOTS]])

        @block.sync
        def _(sp):
            sp.wait_ge(setup_dve, 1)
            sp.dma_start(krow[:, P - 1:P - 1 + L], conv_rows).then_inc(kpad_in, 16)
            sp.dma_start(drow[:], conv_d).then_inc(kpad_in, 16)
            sp.dma_start(xt[0][:], x_t[0]).then_inc(x_in[0], 16)
            sp.dma_start(cx[0][:], ctx_ext[0]).then_inc(ctx_in[0], 16)
            sp.dma_start(gts[:], gates).then_inc(consts_in, 16)
            sp.dma_start(gw[:], gate_w).then_inc(consts_in, 16)
            sp.dma_start(xt[1][:], x_t[1]).then_inc(x_in[1], 16)
            sp.dma_start(cx[1][:], ctx_ext[1]).then_inc(ctx_in[1], 16)
            sp.wait_ge(kpad_ok, 1)
            sp.dma_start(kpad, krow[:]).then_inc(kpad_out, 16)
            sp.wait_ge(kpad_out, 16)
            shared_t = bass.AP(weights.tensor, EXPERTS * P * WROW, [[P * STAGE, TILES], [STAGE, P], [1, STAGE]])

            def load(t, which):
                p = t.odd
                if which == "toep":
                    sp.dma_start(toep[p][:].rearrange("p (h c) -> p h c", h=2),
                                 toeplitz[bass.ds(t.v, 1)].rearrange("x p h c -> (x p) h c")).then_inc(toep_in[p], 16)
                if which == "ctx":
                    sp.dma_start(cx[p][:], ctx_ext[bass.ds(t.v, 1)].rearrange("x p c -> (x p) c")).then_inc(ctx_in[p], 16)
                if which == "x":
                    sp.dma_start(xt[p][:], x_t[bass.ds(t.v, 1)].rearrange("x p c -> (x p) c")).then_inc(x_in[p], 16)
                if which == "xr":
                    sp.dma_start(xr[p][:], x_t[bass.ds(t.v, 1)].rearrange("x p c -> (x p) c")).then_inc(xr_in[p], 16)
                if which == "stage":
                    sp.dma_start(stage[p][:],
                                 shared_t[bass.ds(t.v, 1)].rearrange("x p c -> (x p) c")).then_inc(stage_in[p], 16)

            for t in (At(0), At(1)):
                load(t, "toep")
            for t in (At(0), At(1)):
                load(t, "xr")
                load(t, "stage")

            def turn(t, ahead=True):
                p = t.odd
                if ahead:
                    wait(sp, kv_ok, (t + 1) * 2)
                    load(t + 2, "ctx")
                    wait(sp, xn_ok, t + 1)
                    load(t + 2, "x")
                    wait(sp, slo_ok, t + 1)
                    load(t + 2, "stage")
                    wait(sp, toepl_ok, t + 1)
                    load(t + 2, "toep")
                wait(sp, x2_ok, t + 1)
                sp.dma_start(x2_t[bass.ds(t.v, 1)].rearrange("x p c -> (x p) c"), x2[p][:]).then_inc(x2_out[p], 16)
                if ahead:
                    load(t + 2, "xr")
                wait(sp, t_ok, t + 1)
                sp.dma_start(t_t[bass.ds(t.v, 1)].rearrange("x p c -> (x p) c"), t1[p][:]).then_inc(t_out[p], 16)
                wait(sp, tT_ok, t + 1)
                sp.dma_start(tT_t[bass.ds(t.v, 1)].rearrange("x p c -> (x p) c"), tT[p][:]).then_inc(tT_out[p], 16)

            n = (TILES - 2) // 2
            with sp.Fori(0, n) as i:
                turn(At(0, 2, i, n))
                turn(At(1, 2, i, n))
            turn(At(TILES - 2), False)

            def load_rows(j):
                p = j.odd
                wait(sp, tTl_ok, j - 1)
                sp.dma_start(tn[p][:], tT_t[bass.ds(j.v, 1)].rearrange("x p c -> (x p) c")).then_inc(tn_in[p], 16)
                wait(sp, y_ok, j - 1)
                sp.dma_start(x2in[p][:], x2_t[bass.ds(j.v, 1)].rearrange("x p c -> (x p) c")).then_inc(x2_in[p], 16)

            sp.wait_ge(kv_ok, 2 * TILES)
            sp.wait_ge(toepl_ok, TILES)
            for p in (0, 1):
                sp.wait_ge(tT_out[p], 16)
                sp.wait_ge(x2_out[p], 16)
            load_rows(At(0))
            load_rows(At(1))
            turn(At(TILES - 1), False)
            for p in (0, 1):
                for stored in (x2_out, t_out, tT_out):
                    sp.wait_ge(stored[p], 16 * TILES // 2)

            def store_rows(j):
                p = j.odd
                wait(sp, y_ok, j + 1)
                sp.dma_start(out_t[bass.ds(j.v, 1)].rearrange("x p c -> (x p) c"), ys[p][:]).then_inc(out_ok[p], 16)

            def info(s, field, most):
                return sp.value_load(tile_info[0:1, bass.ds(s.v * INFO + field, 1)], min_val=0, max_val=most)

            LAST_ROW = (EXPERTS - 1) * P

            def load_up(s):
                row, new, half = info(s, 3, LAST_ROW), info(s, 4, 1), info(s, 5, W13)
                for n_ in (0, 1):
                    a, b = PIECE[n_]
                    wait_up(sp, n_, s)
                    wait(sp, lo_ok[n_], s)
                    sp.dma_start(raw_up[:, bass.ds(half + a, b - a)], weights[bass.ds(row, P), a:b],
                                 cond=(new > 0)).then_inc(raw_in[n_][s.odd], 16)

            def load_down(s):
                row, new = info(s, 0, LAST_ROW), info(s, 1, 1)
                wait(sp, lo_ok[2], s)
                sp.dma_start(raw_down[:], weights[bass.ds(row, P), W13:WROW],
                             cond=(new > 0)).then_inc(raw_in[2][s.odd], 16)

            def step(u):
                if u.within(0, UNITS2 - 2 * 2) and u.odd:
                    load_rows((u - 1).half() + 2)
                if shared(u) and u.odd and shared(u - 3) and u.within(3, UNITS2):
                    store_rows((u - 3).half())
                if u.within(UNITS2, UNITS2 + 2) and u.odd:
                    store_rows(At(TILES - 1))
                if u.within(UNITS2 - 3, UNITS2 - 2):
                    sp.wait_ge(r_done, 1)
                    row = info(At(0), 0, LAST_ROW)
                    for n_ in (0, 1):
                        a, b = PIECE[n_]
                        sp.dma_start(raw_up[:, a:b], weights[bass.ds(row, P), a:b]).then_inc(raw_in[n_][1], 16)
                    load_up(At(0))
                    load_down(At(0))
                if routed(u) and routed(u + 2):
                    load_up(u + 1 - UNITS2)
                if routed(u) and routed(u - 1):
                    load_down(u - UNITS2)

            steps(sp, step)
            for p in (0, 1):
                sp.wait_ge(added[p], 16 * ((SLOT_TILES + 1 - p) // 2))
                sp.wait_ge(out_ok[p], 16 * TILES // 2)

        @block.scalar
        def _(act):
            act.wait_ge(consts_in, 32)
            act.activation(small[:, 1:3], gts[:], ACT.Tanh).then_inc(gate_tanh, 1)
            act.wait_ge(setup_dve, 3)

            def std_x(t):
                wait(act, stat1, (t + 1) * 2)
                act.activation(sd1[t.odd][:, 0:1], mv1[t.odd][:, 1:2], ACT.Sqrt, bias=small[:, 0:1]).then_inc(std1, 1)

            def std_x2(t):
                wait(act, stat2, (t + 1) * 2)
                act.activation(sd2[t.odd][:, 0:1], mv2[t.odd][:, 1:2], ACT.Sqrt, bias=small[:, 0:1]).then_inc(std2, 1)

            def q_copy(t):
                p = t.odd
                wait(act, prod_ok, (t - 1) * 24)
                wait(act, q_turned, t + 1)
                src = ps_q[:].rearrange("p (l c) -> p l c", l=BLOCKS)
                dst = q[p][:].rearrange("p (l c) -> p l c", l=BLOCKS)
                act.activation(dst[:, :, 0:P], src, ACT.Copy).then_inc(q_ok, 1)
                act.activation(dst[:, :, P:], src[:, :, 0:GROUPS * EXT - P], ACT.Copy).then_inc(q_ok, 1)

            def tT_copy(t):
                wait(act, t_turned, t + 1)
                wait(act, tT_out[t.odd], t.half() * 16)
                wait(act, gate_ok, t - 1)
                act.activation(tT[t.odd][:], ps_t[:], ACT.Copy).then_inc(tT_ok, 1)

            def split_conv(t):
                p = t.odd
                wait(act, conv_ok, (t - 1) * 8)
                wait(act, toep_in[p], (t.half() + 1) * 16)
                act.activation(toep_hi[p][:], toep[p][:], ACT.Copy).then_inc(toeph_ok, 1)
                wait(act, kv_ok, (t + 1) * 2)
                act.activation(kv_hi[p][:], kv[:], ACT.Copy).then_inc(kvh_ok, 1)

            def split_shared(t):
                p = t.odd
                wait(act, stage_in[p], (t.half() + 1) * 16)
                act.activation(shared_hi[:, bass.ds(t.v * STAGE, STAGE)], stage[p][:], ACT.Copy).then_inc(shi_ok, 1)

            std_x(At(0))
            split_conv(At(0))
            q_copy(At(0))

            def turn(t):
                if not t.within(0, 1):
                    std_x2(t - 1)
                if not t.within(TILES - 1, TILES):
                    std_x(t + 1)
                split_shared(t)
                if not t.within(TILES - 1, TILES):
                    split_conv(t + 1)
                if not t.within(0, 1):
                    tT_copy(t - 1)
                if not t.within(TILES - 1, TILES):
                    q_copy(t + 1)

            pairs(act, turn)

            def tile_hi(j):
                if j.within(0, TILES):
                    wait(act, tn_in[j.odd], (j.half() + 1) * 16)
                    wait(act, up_ok, (j - 1) * 2)
                    act.activation(tT_hi[j.odd][:], tn[j.odd][:], ACT.Copy).then_inc(tTh_ok, 1)
                else:
                    wait(act, tile_turned, j - TILES + 1)
                    act.activation(tT_hi[j.odd][:], ps_t[:], ACT.Copy).then_inc(tTh_ok, 1)

            def step(u):
                s = u - UNITS2
                if routed(u - 3):
                    v = u - 3
                    wait(act, down_ok, v + 1)
                    wait(act, added[v.odd], (v - UNITS2).half() * 16)
                    wait(act, sidx_ok, v - UNITS2 + 1)
                    if v.within(UNITS2, UNITS2 + 2):
                        wait(act, out_ok[v.odd], 16 * TILES // 2)
                    act.activation(ys[v.odd][:], ps_y[:], ACT.Copy,
                                   scale=sca_i[v.odd][:, 2:3].bitcast(F32)).then_inc(yr_ok, 1)
                if routed(u + 1):
                    v = u + 1
                    half = half_of(act, v - UNITS2)
                    for n_ in (0, 1):
                        a, b = PIECE[n_]
                        wait_up(act, n_, v - UNITS2)
                        wait(act, up_ok, v - 1)
                        c = 1 + n_ + 2 * v.odd
                        act.activation(ahop[:, c:c + 1], ahop[:, 0:1], ACT.Copy)
                        act.activation(w_hi[v.odd][:, a:b], raw_up[:, bass.ds(half + a, b - a)],
                                       ACT.Copy).then_inc(hi_ok[n_], 1)
                if shared(u) or routed(u):
                    wait(act, hid_ok, u)
                    wait(act, up_ok, u + 1)
                    act.activation(silu[:], ps_h1[:, 0:INTER], ACT.Silu).then_inc(silu_ok, 1)
                v = u - 1
                if shared(v) or routed(v):
                    wait(act, down_ok, v - 1)
                    wait(act, hid_turned, v + 1)
                    act.activation(hT_hi[v.odd][:], ps_ht[:, 0:IPAD], ACT.Copy).then_inc(hTh_ok, 1)
                for j in turned_at(u):
                    tile_hi(j)

            tile_hi(At(0))
            std_x2(At(TILES - 1))

            def after(u):
                if u == 0:
                    tT_copy(At(TILES - 1))
                if u == 3:
                    act.wait_ge(rt, R_EXP)
                    act.activation(lex[:], lex[:], ACT.Exp).then_inc(r_exp, 1)

            steps(act, step, after)

        @block.vector
        def _(dve):
            dve.memset(krow[:], 0.0).then_inc(setup_dve, 1)
            dve.memset(small[:, 0:1], EPS).then_inc(setup_dve, 1)
            dve.memset(ahop[:], 0.0).then_inc(setup_dve, 1)
            dve.memset(hop[:], 0.0).then_inc(setup_dve, 1)
            dve.wait_ge(kpad_in, 32)
            dve.tensor_tensor(krow[:, P - 1:P], krow[:, P - 1:P], drow[:], ALU.add).then_inc(kpad_ok, 1)
            dve.memset(prod[0][:], 0.0).then_inc(setup_dve, 1)
            dve.memset(prod[1][:], 0.0).then_inc(setup_dve, 1)
            dve.wait_ge(setup_dve, 6)

            def stats(src, st, mv, ok, t):
                p = t.odd
                dve.bn_stats(st[p][:], src[p][:]).then_inc(ok, 1)
                wait(dve, ok, t * 2 + 1)
                dve.tensor_copy(hop[:, 1:2], hop[:, 0:1])
                dve.bn_aggr(mv[p][:], st[p][:]).then_inc(ok, 1)

            def stats_x(t):
                dve.wait_ge(setup_dve, 1)
                wait(dve, x_in[t.odd], (t.half() + 1) * 16)
                stats(xt, st1, mv1, stat1, t)

            def norm_x(t):
                p = t.odd
                wait(dve, std1, t + 1)
                dve.reciprocal(sd1[p][:, 1:2], sd1[p][:, 0:1]).then_inc(rstd1, 1)
                wait(dve, q_turned, t - 1)
                wait(dve, rstd1, t + 1)
                dve.tensor_scalar(xn[p][:], xt[p][:], mv1[p][:, 0:1], sd1[p][:, 1:2],
                                  ALU.subtract, ALU.mult).then_inc(xn_ok, 1)

            def residual(t):
                p = t.odd
                wait(dve, x2_out[p], t.half() * 16)
                wait(dve, xr_in[p], (t.half() + 1) * 16)
                wait(dve, summed, (t + 1) * 4)
                dve.scalar_tensor_tensor(x2[p][:], ps_o[:], small[:, 1:2], xr[p][:],
                                         ALU.mult, ALU.add).then_inc(x2_ok, 1)
                wait(dve, x2_ok, t + 1)
                stats(x2, st2, mv2, stat2, t)

            def norm_x2(t):
                p = t.odd
                wait(dve, std2, t + 1)
                dve.reciprocal(sd2[p][:, 1:2], sd2[p][:, 0:1]).then_inc(rstd2, 1)
                wait(dve, t_out[p], t.half() * 16)
                wait(dve, t_turned, t - 1)
                wait(dve, rstd2, t + 1)
                dve.tensor_scalar(t1[p][:], x2[p][:], mv2[p][:, 0:1], sd2[p][:, 1:2],
                                  ALU.subtract, ALU.mult).then_inc(t_ok, 1)

            def products(t, lb):
                par = lb % 2
                G, HB = GROUPS, HD * BATCH
                for h in range(2):
                    y = ps_conv[par][h][:]
                    qo = lb * GROUPS * EXT + h * BATCH
                    po = h * BATCH
                    qq, pp = q[t.odd][:], prod[par][:]
                    if h == 0:
                        wait(dve, summed, t * 4 + lb - 1)
                        if lb == 0:
                            wait(dve, q_ok, (t + 1) * 2)
                    wait(dve, conv_ok, t * 8 + 2 * lb + h + 1)
                    dve.tensor_tensor(view(pp, po, [[P + G, 4], [G, HD], [1, BATCH]]),
                                      view(y, 0, [[HB, 4], [BATCH, HD], [1, BATCH]]),
                                      view(qq, qo, [[0, 4], [G, HD], [1, BATCH]]), ALU.mult).then_inc(prod_ok, 1)
                    dve.tensor_tensor(view(pp, po + 5 * P, [[P, 3], [G, HD], [1, BATCH]]),
                                      view(y, HB, [[HB, 3], [BATCH, HD], [1, BATCH]]),
                                      view(qq, qo + G, [[G, 3], [G, HD], [1, BATCH]]), ALU.mult).then_inc(prod_ok, 1)
                    dve.tensor_tensor(view(pp, po + 8 * P, [[4 * G, 2], [G, 4], [1, BATCH]]),
                                      view(y, 4 * HB, [[0, 2], [BATCH, 4], [1, BATCH]]),
                                      view(qq, qo + 4 * G, [[4 * G, 2], [G, 4], [1, BATCH]]), ALU.mult).then_inc(prod_ok, 1)

            def split_kv(t):
                wait(dve, kvh_ok, t + 1)
                dve.tensor_tensor(kv_lo[t.odd][:, 0:KV_DVE], kv[:, 0:KV_DVE], kv_hi[t.odd][:, 0:KV_DVE].bitcast(F32),
                                  ALU.subtract).then_inc(kvl_ok, 1)

            def logits_copy(t):
                wait(dve, gate_ok, t + 1)
                dve.tensor_scalar(logits[:, bass.ds(t.v * EXPERTS, EXPERTS)], ps_gate[:, 0:EXPERTS], 1.0, None,
                                  ALU.mult).then_inc(logits_ok, 1)

            stats_x(At(0))
            form(dve, At(0))
            norm_x(At(0))
            split_kv(At(0))
            dve.wait_ge(gate_tanh, 1)

            def turn(t):
                first, last = t.within(0, 1), t.within(TILES - 1, TILES)
                products(t, 0)
                if not first:
                    residual(t - 1)
                if not last:
                    stats_x(t + 1)
                products(t, 1)
                if not first:
                    norm_x2(t - 1)
                if not last:
                    norm_x(t + 1)
                products(t, 2)
                if not last:
                    split_kv(t + 1)
                products(t, 3)
                if not first:
                    logits_copy(t - 1)

            pairs(dve, turn)

            def tile_lo(j):
                wait(dve, tTh_ok, j + 1)
                src = tn[j.odd] if j.within(0, TILES) else ps_t
                dve.tensor_tensor(tT_lo[j.odd][:], src[:], tT_hi[j.odd][:].bitcast(F32),
                                  ALU.subtract).then_inc(tTl_ok, 1)

            tile_lo(At(0))
            residual(At(TILES - 1))
            norm_x2(At(TILES - 1))
            dve.wait_ge(slo_ok, TILES)
            dve.wait_ge(conv_ok, 8 * TILES)
            dve.memset(hid[0][:, INTER:IPAD], 0.0).then_inc(hid_zero, 1)
            dve.memset(hid[1][:, INTER:IPAD], 0.0).then_inc(hid_zero, 1)
            dve.wait_ge(hid_zero, 2)

            def step(u):
                if routed(u + 1):
                    v = u + 1
                    half = half_of(dve, v - UNITS2)
                    for n_ in (0, 1):
                        a, b = PIECE[n_]
                        wait(dve, hi_ok[n_], v - UNITS2 + 1)
                        dve.tensor_tensor(w_lo[v.odd][:, a:b], raw_up[:, bass.ds(half + a, b - a)], w_hi[v.odd][:, a:b].bitcast(F32),
                                          ALU.subtract).then_inc(lo_ok[n_], 1)
                if shared(u) or routed(u):
                    wait(dve, hid_turned, u - 1)
                    wait(dve, silu_ok, u + 1)
                    dve.tensor_tensor(hid[u.odd][:, 0:INTER], silu[:], ps_h3[:, 0:INTER], ALU.mult).then_inc(hid_ok, 1)
                v = u - 1
                if shared(v) or routed(v):
                    wait(dve, hTh_ok, v + 1)
                    dve.tensor_tensor(hT_lo[v.odd][:], ps_ht[:, 0:IPAD], hT_hi[v.odd][:].bitcast(F32),
                                      ALU.subtract).then_inc(hTl_ok, 1)
                for j in turned_at(u):
                    tile_lo(j)
                if routed(u - 1):
                    v = u - 1
                    a, b = PIECE[2]
                    wait(dve, raw_in[2][v.odd], ((v - UNITS2).half() + 1) * 16)
                    wait(dve, down_ok, v - 1)
                    dve.tensor_copy(w_hi[v.odd][:, a:b], raw_down[:]).then_inc(hi_ok[2], 1)
                if u.within(3, UNITS2 + 2) and u.odd:
                    j = (u - 3).half()
                    wait(dve, x2_in[j.odd], (j.half() + 1) * 16)
                    wait(dve, out_ok[j.odd], j.half() * 16)
                    wait(dve, down_ok, (j + 1) * 2)
                    dve.scalar_tensor_tensor(ys[j.odd][:], ps_y[:], small[:, 2:3], x2in[j.odd][:],
                                             ALU.mult, ALU.add).then_inc(y_ok, 1)

            count = [0]

            def did(ins):
                count[0] += 1
                ins.then_inc(rt, 1)

            def chain():
                dve.wait_ge(rt, count[0])

            def b3(t_, dims):
                return view(t_, 0, dims)

            E_, T_ = EXPERTS, TILES

            def pick_experts(tiles):
                for t in tiles:
                    did(dve.max(mx[:, t, :], logits[:, t * E_:(t + 1) * E_]))
                chain()
                for t in tiles:
                    did(dve.max_index(mi[:, t, :], mx[:, t, :], logits[:, t * E_:(t + 1) * E_]))

            def masks():
                chain()
                assert count[0] == R_PICK
                for k in range(2):
                    did(dve.tensor_copy(pick[:, k, :], mi[:, :, k]))
                chain()
                for k in range(2):
                    did(dve.tensor_tensor(mask[k][:], view(io[:], 0, [[0, T_], [1, E_]]),
                                          view(pick[:, k, :], 0, [[1, T_], [0, E_]]), ALU.is_equal))
                did(dve.tensor_tensor(lex[:, :, 0:E_], logits[:].rearrange("p (t e) -> p t e", e=E_),
                                      view(mx[:], 0, [[8, T_], [0, E_]]), ALU.subtract))
                did(dve.tensor_tensor(lex[:, :, E_:E_ + 1], mx[:, :, 1:2], mx[:, :, 0:1], ALU.subtract))
                chain()
                did(dve.tensor_tensor(both[:], mask[0][:], mask[1][:], ALU.add))
                assert count[0] == R_EXP
                dve.wait_ge(rt, count[0])
                dve.tensor_copy(hop[:, 1:2], hop[:, 0:1]).then_inc(r_both, 1)

            def softmax_weights():
                dve.wait_ge(r_exp, 1)
                did(dve.tensor_reduce(ssum[:], lex[:, :, 0:E_], AX.X, ALU.add))
                chain()
                did(dve.reciprocal(ssum[:], ssum[:]))
                chain()
                did(dve.tensor_scalar(wts[:, 0, :], ssum[:], small[:, 2:3], None, ALU.mult))
                chain()
                did(dve.tensor_tensor(wts[:, 1, :], lex[:, :, E_], wts[:, 0, :], ALU.mult))
                chain()
                flat = wts[:].rearrange("p k t -> p (k t)")
                did(dve.tensor_copy(wpart[:, 0, :], flat))
                chain()
                did(dve.tensor_tensor(wres[:], flat, wpart[:, 0, :], ALU.subtract))
                chain()
                did(dve.tensor_copy(wpart[:, 1, :], wres[:]))
                chain()
                did(dve.tensor_tensor(wres[:], wres[:], wpart[:, 1, :], ALU.subtract))
                chain()
                dve.tensor_copy(wpart[:, 2, :], wres[:]).then_inc(r_weights, 1)

            def rows_of_experts():
                dve.wait_ge(r_count, 1)
                chain()
                did(dve.tensor_copy(cum[0][:], ps_total[:, 0:T_ * E_].rearrange("p (t e) -> p t e", e=E_)))
                for n_ in range(4):
                    d, src, dst = 1 << n_, cum[n_ % 2], cum[1 - n_ % 2]
                    chain()
                    did(dve.tensor_copy(dst[:, 0:d, :], src[:, 0:d, :]))
                    did(dve.tensor_tensor(dst[:, d:, :], src[:, d:, :], src[:, 0:T_ - d, :], ALU.add))

            def tiles_of_experts():
                chain()
                did(dve.tensor_tensor(cmp[:], view(cum[0][:, T_ - 1, :], 0, [[1, E_], [0, T_]]),
                                      view(tcmp[:], 0, [[0, E_], [1, T_]]), ALU.is_gt))
                chain()
                did(dve.tensor_reduce(ntile_own[:], cmp[:], AX.X, ALU.add))
                chain()
                did(dve.tensor_copy(ntile[0][:], ntile_own[:]))
                for n_ in range(4):
                    d, src, dst = 1 << n_, ntile[n_ % 2], ntile[1 - n_ % 2]
                    chain()
                    did(dve.tensor_copy(dst[:, 0:d], src[:, 0:d]))
                    did(dve.tensor_tensor(dst[:, d:], src[:, d:], src[:, 0:E_ - d], ALU.add))
                chain()
                did(dve.tensor_tensor(ntile[1][:], ntile[0][:], ntile_own[:], ALU.subtract))
                chain()
                did(dve.tensor_scalar(ntile[1][:], ntile[1][:], float(P), None, ALU.mult))

            def slots():
                chain()
                did(dve.tensor_copy(cum[1][:, 0, :], ntile[1][:]))
                did(dve.tensor_tensor(cum[1][:, 1:, :], cum[0][:, 0:T_ - 1, :],
                                      view(ntile[1][:], 0, [[0, T_ - 1], [1, E_]]), ALU.add))
                chain()
                did(dve.tensor_tensor(cum[0][:], ps_rank[:, 0:T_ * E_].rearrange("p (t e) -> p t e", e=E_),
                                      cum[1][:], ALU.add))
                chain()
                for k in range(2):
                    did(dve.tensor_tensor(mask[k][:], mask[k][:], cum[0][:], ALU.mult))
                chain()
                for k in range(2):
                    did(dve.tensor_reduce(slot[:, k * T_:(k + 1) * T_], mask[k][:], AX.X, ALU.add))
                chain()
                did(dve.tensor_copy(sloti[:, 0, :], slot[:]))
                chain()
                did(dve.tensor_scalar(sloti[:, 1, :], sloti[:, 0, :], 7, None, ALU.logical_shift_right))
                did(dve.tensor_scalar(sloti[:, 2, :], sloti[:, 0, :], P - 1, None, ALU.bitwise_and))
                chain()
                dve.tensor_copy(slotb[:], sloti[:, 1:3, :]).then_inc(rt, 1)
                count[0] += 1

            def tiles_of_choices():
                chain()
                dve.tensor_tensor(field_of(2), view(iob[:], 0, [[0, NK], [1, SLOTS]]),
                                  view(slotb[:, 0, :], 0, [[1, NK], [0, SLOTS]]), ALU.is_equal).then_inc(r_tiles, 1)

            def places(part):
                n, n0 = NK // 4, part * NK // 4
                dve.tensor_tensor(place[:, n0:n0 + n, :], view(iob[:], 0, [[0, n], [1, P]]),
                                  view(slotb[:, 1, :], n0, [[1, n], [0, P]]), ALU.is_equal).then_inc(r_places, 1)

            ti = tile_info[:].rearrange("p (s k) -> p s k", k=INFO)

            def expert_of_tiles():
                chain()
                did(dve.tensor_tensor(tcmp[:], view(ntile[0][:], 0, [[0, SLOTS], [1, E_]]),
                                      view(io[:], 0, [[1, SLOTS], [0, E_]]), ALU.is_le))
                chain()
                did(dve.tensor_reduce(texp[:, 1:], tcmp[:], AX.X, ALU.add))
                chain()
                did(dve.tensor_scalar(texp[:, 1:], texp[:, 1:], float(E_ - 1), float(P), ALU.min, ALU.mult))
                chain()
                did(dve.tensor_tensor(tmpf[:], texp[:, 1:], texp[:, 0:SLOTS], ALU.not_equal))
                did(dve.tensor_copy(ti[:, :, 0], texp[:, 1:]))
                chain()
                did(dve.tensor_copy(ti[:, :, 1], tmpf[:]))

            def halves_of_tiles():
                did(dve.tensor_scalar(ntile_own[:], ntile_own[:], 0.0, None, ALU.is_gt))
                chain()
                did(dve.tensor_tensor(tcmp[:], tcmp[:], view(ntile_own[:], 0, [[0, SLOTS], [1, E_]]), ALU.mult))
                chain()
                did(dve.tensor_reduce(tnum[:], tcmp[:], AX.X, ALU.add))
                chain()
                did(dve.tensor_copy(inum[:], tnum[:]))
                chain()
                did(dve.tensor_scalar(inum[:], inum[:], 1, None, ALU.bitwise_and))
                chain()
                did(dve.tensor_copy(tnum[:], inum[:]))
                chain()
                did(dve.tensor_scalar(ti[:, :, 2], tnum[:], float(W13), None, ALU.mult))
                did(dve.tensor_scalar(ti[:, :, 5], tnum[:], -float(W13), float(W13), ALU.mult, ALU.add))

            def experts_behind():
                chain()
                did(dve.tensor_scalar(ntile[0][:], ntile_own[:], -64.0, 64.0, ALU.mult, ALU.add))
                did(dve.tensor_scalar(tnum[:], io[:, 0:SLOTS], float(P), None, ALU.mult))
                chain()
                did(dve.tensor_tensor(ntile[0][:], ntile[0][:], io[:, 0:E_], ALU.add))
                did(dve.tensor_tensor(tcmp[:], view(ntile[1][:], 0, [[0, SLOTS], [1, E_]]),
                                      view(tnum[:], 0, [[1, SLOTS], [0, E_]]), ALU.is_le))
                chain()
                did(dve.tensor_scalar(tcmp[:], tcmp[:], 64.0, None, ALU.mult))

            def next_experts():
                chain()
                did(dve.tensor_tensor(tcmp[:], tcmp[:], view(ntile[0][:], 0, [[0, SLOTS], [1, E_]]), ALU.add))
                chain()
                did(dve.tensor_reduce(tnum[:], tcmp[:], AX.X, ALU.min))
                chain()
                did(dve.tensor_scalar(texp[:, 1:], tnum[:], float(E_), None, ALU.is_lt))
                did(dve.tensor_scalar(ti[:, :, 3], tnum[:], float(E_ - 1), float(P), ALU.min, ALU.mult))
                chain()
                did(dve.tensor_tensor(ti[:, :, 4], texp[:, 1:], tmpf[:], ALU.mult))

            def tables():
                dve.wait_ge(r_table, 1)
                chain()
                did(dve.tensor_copy(tab[:], ps_table[:, 0:FIELDS * SLOTS].rearrange("p (f s) -> p f s", s=SLOTS)))
                chain()
                si = slot_info[:].rearrange("p (s k) -> p s k", k=3)
                sf = slot_info[:].bitcast(F32).rearrange("p (s k) -> p s k", k=3)
                did(dve.scalar_tensor_tensor(tab[:, 0, :], tab[:, 0, :], float(P), tab[:, 1, :], ALU.mult, ALU.add))
                did(dve.tensor_scalar(tab[:, 2, :], tab[:, 2, :], -float(SKIP), float(SKIP), ALU.mult, ALU.add))
                did(dve.tensor_tensor(tab[:, 4, :], tab[:, 4, :], tab[:, 5, :], ALU.add))
                chain()
                did(dve.tensor_copy(si[:, :, 0], tab[:, 0, :]))
                did(dve.tensor_tensor(tab[:, 2, :], tab[:, 2, :], tab[:, 0, :], ALU.add))
                did(dve.tensor_tensor(sf[:, :, 2], tab[:, 3, :], tab[:, 4, :], ALU.add))
                chain()
                did(dve.tensor_copy(si[:, :, 1], tab[:, 2, :]))
                chain()
                dve.tensor_copy(hop[:, 1:2], hop[:, 0:1]).then_inc(r_done, 1)

            def after(u):
                if u == 0:
                    logits_copy(At(TILES - 1))
                    dve.wait_ge(logits_ok, TILES)
                    dve.wait_ge(r_const, 1)
                    dve.memset(texp[:, 0:1], -1.0).then_inc(rt, 1)
                    count[0] += 1
                    did(dve.tensor_scalar(tcmp[:, 0, 0:T_], io[:, 0:T_], float(P), None, ALU.mult))
                    pick_experts(range(T_))
                if u == 1:
                    masks()
                if u == 3:
                    rows_of_experts()
                if u == 4:
                    tiles_of_experts()
                if u == 5:
                    slots()
                if u == 6:
                    softmax_weights()
                if u == 7:
                    tiles_of_choices()
                    places(0)
                if u == 8:
                    places(1)
                    places(2)
                if u == 9:
                    places(3)
                if u == 10:
                    expert_of_tiles()
                if u == 11:
                    halves_of_tiles()
                if u == 12:
                    experts_behind()
                if u == 13:
                    next_experts()
                if u == 15:
                    tables()

            steps(dve, step, after)

        @block.tensor
        def _(pe):
            pe.wait_ge(setup_pool, 2)

            def turn_rows(src, dst, ok):
                for c in range(BLOCKS):
                    last = pe.transpose(dst[:, c * P:(c + 1) * P], src[:, c * P:(c + 1) * P], ident[:])
                last.then_inc(ok, 1)

            def turn_q(t):
                wait(pe, q_ok, t * 2)
                wait(pe, xn_ok, t + 1)
                turn_rows(xn[t.odd], ps_q, q_turned)

            def turn_t(t):
                wait(pe, tT_ok, t)
                wait(pe, t_ok, t + 1)
                turn_rows(t1[t.odd], ps_t, t_turned)

            def gate(t):
                wait(pe, logits_ok, t)
                wait(pe, tT_ok, t + 1)
                for c in range(BLOCKS):
                    last = pe.matmul(ps_gate[:, 0:EXPERTS], tT[t.odd][:, c * P:(c + 1) * P],
                                     gw[:, c * EXPERTS:(c + 1) * EXPERTS], start=(c == 0), stop=(c == BLOCKS - 1))
                last.then_inc(gate_ok, 1)

            def conv(t, lb):
                p = t.odd
                n = BATCH * PAIRS
                for h in range(2):
                    if h == 0:
                        if lb == 0:
                            wait(pe, toepl_ok, t + 1)
                            wait(pe, kvl_ok, t + 1)
                            wait(pe, kvl2_ok, t + 1)
                        wait(pe, prod_ok, (t * 4 + lb - 1) * 6)
                    for mb in range(lb + 1):
                        d = lb - mb
                        o = (mb * 2 + h) * n
                        k = h * L + d * P
                        for m, (w, z) in enumerate(((toep_hi, kv_hi), (toep_hi, kv_lo), (toep_lo, kv_hi))):
                            mm = pe.matmul(ps_conv[lb % 2][h][:, 0:n], w[p][:, k:k + P], z[p][:, o:o + n],
                                           start=(mb == 0 and m == 0), stop=(mb == lb and m == 2))
                    mm.then_inc(conv_ok, 1)

            def sum_rows(t, lb):
                if lb == 0:
                    wait(pe, x2_ok, t)
                wait(pe, prod_ok, (t * 4 + lb + 1) * 6)
                for r in range(SUMROWS):
                    mm = pe.matmul(ps_o[:, lb * P:(lb + 1) * P],
                                   prod[lb % 2][:, r * P:(r + 1) * P], ident[:],
                                   is_transpose=True, start=(r == 0), stop=(r == SUMROWS - 1))
                mm.then_inc(summed, 1)

            turn_q(At(0))

            def turn(t):
                first, last = t.within(0, 1), t.within(TILES - 1, TILES)
                conv(t, 0)
                if not first:
                    sum_rows(t - 1, 3)
                conv(t, 1)
                sum_rows(t, 0)
                conv(t, 2)
                sum_rows(t, 1)
                if not first:
                    turn_t(t - 1)
                if not last:
                    turn_q(t + 1)
                conv(t, 3)
                if not first:
                    gate(t - 1)
                sum_rows(t, 2)

            pairs(pe, turn)
            sum_rows(At(TILES - 1), 3)

            def turn_tile(j):
                wait(pe, row_in[j.odd], ((j - TILES).half() + 1) * 16)
                wait(pe, tTl_ok, j)
                turn_rows(tn[j.odd], ps_t, tile_turned)

            def parts(hi, lo, whi, wlo):
                return (hi, whi), (hi, wlo), (lo, whi)

            def up(u):
                j = tile_of(u)
                wait(pe, hid_ok, u)
                if shared(u):
                    whi, wlo, o = shared_hi, shared_lo, u.odd * WROW
                    wait(pe, slo_ok, TILES)
                else:
                    whi, wlo, o = w_hi[u.odd], w_lo[u.odd], 0
                    wait(pe, lo_ok[0], u - UNITS2 + 1)
                    wait(pe, lo_ok[1], u - UNITS2 + 1)
                wait(pe, tTl_ok, j + 1)
                for c in range(BLOCKS):
                    for k, (a, w) in enumerate(parts(tT_hi[j.odd], tT_lo[j.odd], whi, wlo)):
                        for n_, dst in enumerate((ps_h1, ps_h3)):
                            f = o + (c * 2 + n_) * INTER
                            mm = pe.matmul(dst[:, 0:INTER], a[:, c * P:(c + 1) * P], w[:, f:f + INTER],
                                           start=(c == 0 and k == 0), stop=(c == BLOCKS - 1 and k == 2))
                mm.then_inc(up_ok, 1)

            def turn_hidden(u):
                wait(pe, hTl_ok, u)
                wait(pe, hid_ok, u + 1)
                for c in range(ICH):
                    last = pe.transpose(ps_ht[:, c * P:(c + 1) * P], hid[u.odd][:, c * P:(c + 1) * P], ident[:])
                last.then_inc(hid_turned, 1)

            def down(u):
                if shared(u):
                    whi, wlo, o = shared_hi, shared_lo, u.odd * WROW + W13
                    if not u.odd:
                        wait(pe, y_ok, u.half())
                    first, last = not u.odd, bool(u.odd)
                else:
                    whi, wlo, o = w_hi[u.odd], w_lo[u.odd], W13
                    if u.within(UNITS2, UNITS2 + 1):
                        wait(pe, y_ok, TILES)
                    wait(pe, yr_ok, u - UNITS2)
                    wait(pe, hi_ok[2], u - UNITS2 + 1)
                    wait(pe, lo_ok[2], u - UNITS2 + 1)
                    first = last = True
                wait(pe, hTl_ok, u + 1)
                for c in range(ICH):
                    for k, (a, w) in enumerate(parts(hT_hi[u.odd], hT_lo[u.odd], whi, wlo)):
                        mm = pe.matmul(ps_y[:], a[:, c * P:(c + 1) * P], w[:, o + c * L:o + (c + 1) * L],
                                       start=(first and c == 0 and k == 0), stop=(last and c == ICH - 1 and k == 2))
                mm.then_inc(down_ok, 1)

            def step(u):
                if shared(u) or routed(u):
                    up(u)
                if shared(u - 1) or routed(u - 1):
                    turn_hidden(u - 1)
                for j in turned_at(u):
                    if not j.within(0, TILES):
                        turn_tile(j)
                if shared(u - 2) or routed(u - 2):
                    down(u - 2)

            def after(u):
                if u == 0:
                    turn_t(At(TILES - 1))
                    gate(At(TILES - 1))
                if u == 2:
                    pe.wait_ge(r_both, 1)
                    pe.wait_ge(x2_ok, TILES)
                    pe.wait_ge(q_ok, 2 * TILES)
                    n = TILES * EXPERTS
                    flat = both[:].rearrange("p t e -> p (t e)")
                    pe.matmul(ps_rank[:, 0:n], upper[:], flat, start=True, stop=True)
                    pe.matmul(ps_total[:, 0:n], ones[:], flat, start=True, stop=True).then_inc(r_count, 1)
                if u == 14:
                    pe.wait_ge(r_fields, 5)
                    pe.wait_ge(r_places, 4)
                    for k in range(2 * TILES):
                        mm = pe.matmul(ps_table[:, 0:FIELDS * SLOTS], place[:, k, :],
                                       field[:, k, :, :].rearrange("p f s -> p (f s)"),
                                       start=(k == 0), stop=(k == 2 * TILES - 1))
                    mm.then_inc(r_table, 1)

            steps(pe, step, after)

        @block.gpsimd
        def _(pool):
            pool.iota(slot_info[:, 0:P].bitcast(F32), [[1, P]], base=0, channel_multiplier=-1,
                      allow_small_or_imprecise_dtypes=True).then_inc(setup_pool, 1)
            pool.wait_ge(setup_pool, 1)
            pool.tensor_scalar(ident[:], slot_info[:, 0:P].bitcast(F32), 0.0, None, ALU.is_equal).then_inc(setup_pool, 1)

            def split_shared(t):
                p = t.odd
                o = t * STAGE
                wait(pool, shi_ok, t + 1)
                pool.tensor_tensor(shared_lo[:, bass.ds(o.v, STAGE)], stage[p][:],
                                   shared_hi[:, bass.ds(o.v, STAGE)].bitcast(F32), ALU.subtract).then_inc(slo_ok, 1)

            def split_toep(t):
                p = t.odd
                wait(pool, toeph_ok, t + 1)
                pool.tensor_tensor(toep_lo[p][:], toep[p][:], toep_hi[p][:].bitcast(F32),
                                   ALU.subtract).then_inc(toepl_ok, 1)

            def split_kv(t):
                wait(pool, kvh_ok, t + 1)
                pool.tensor_tensor(kv_lo[t.odd][:, KV_DVE:], kv[:, KV_DVE:], kv_hi[t.odd][:, KV_DVE:].bitcast(F32),
                                   ALU.subtract).then_inc(kvl2_ok, 1)

            split_kv(At(0))
            split_toep(At(0))

            def turn(t):
                if not t.within(TILES - 1, TILES):
                    form(pool, t + 1)
                split_shared(t)
                if not t.within(TILES - 1, TILES):
                    split_toep(t + 1)
                    split_kv(t + 1)

            pairs(pool, turn)
            pool.wait_ge(conv_ok, 8 * TILES)
            pool.wait_ge(summed, 4 * TILES)
            pool.wait_ge(gate_ok, TILES)
            pool.wait_ge(t_ok, TILES)
            for p in (0, 1):
                pool.wait_ge(x2_out[p], 16 * TILES // 2)
            pool.iota(io[:], [[1, P]], base=0, channel_multiplier=0,
                      allow_small_or_imprecise_dtypes=True).then_inc(setup_pool, 1)
            pool.iota(place[:, 0, :], [[1, P]], base=0, channel_multiplier=-1,
                      allow_small_or_imprecise_dtypes=True).then_inc(setup_pool, 1)
            pool.iota(trow[:], [[0, 2], [1, TILES]], base=0, channel_multiplier=0,
                      allow_small_or_imprecise_dtypes=True).then_inc(setup_pool, 1)
            pool.iota(prow[:], [[0, 2 * TILES]], base=0, channel_multiplier=1,
                      allow_small_or_imprecise_dtypes=True).then_inc(setup_pool, 1)
            pool.memset(ones[:], 1.0).then_inc(setup_pool, 1)
            pool.memset(phop[:], 0.0).then_inc(setup_pool, 1)
            pool.wait_ge(setup_pool, 8)
            pool.tensor_copy(iob[:], io[:]).then_inc(setup_pool, 1)
            pool.tensor_scalar(upper[:], place[:, 0, :], 0.0, None, ALU.is_gt).then_inc(setup_pool, 1)
            pool.wait_ge(setup_pool, 10)
            pool.memset(pid[:], 0.0).then_inc(r_const, 1)

            def hold(n):
                pool.tensor_tensor(phop[:, n:n + 1], phop[:, 0:1], phop[:, 0:1], ALU.add)

            def gather(s):
                p = s.odd
                if s.within(0, 2):
                    wait(pool, tTl_ok, s + TILES - 1)
                wait(pool, tile_turned, s - 1)
                wait(pool, row_in[p], s.half() * 16)
                pool.tensor_copy(gat_i[p][:], slot_info[:, bass.ds(s.v * 3, 3)]).then_inc(gidx_ok, 1)
                wait(pool, gidx_ok, s + 1)
                hold(1 + p)
                pool.indirect_dma_start(out=tn[p][:], out_offset=None, in_=t_rows,
                                        in_offset=bass.IndirectOffsetOnAxis(ap=gat_i[p][:, 0:1], axis=0),
                                        bounds_check=ROWS - 1, oob_is_err=False).then_inc(row_in[p], 16)

            def scatter(s):
                p = s.odd
                if s.within(0, 1):
                    for k in (0, 1):
                        pool.wait_ge(out_ok[k], 16 * TILES // 2)
                wait(pool, yr_ok, s + 1)
                prev = s - 1
                if not s.within(0, 1):
                    wait(pool, added[prev.odd], (prev.half() + 1) * 16)
                hold(3 + p)
                pool.indirect_dma_start(out=out, out_offset=bass.IndirectOffsetOnAxis(ap=sca_i[p][:, 1:2], axis=0),
                                        in_=ys[p][:], in_offset=None, bounds_check=ROWS - 1, oob_is_err=False,
                                        compute_op=ALU.add).then_inc(added[p], 16)

            def scatter_index(s):
                p = s.odd
                wait(pool, added[p], s.half() * 16)
                pool.tensor_copy(sca_i[p][:], slot_info[:, bass.ds(s.v * 3, 3)]).then_inc(sidx_ok, 1)

            def step(u):
                s = u - UNITS2
                if routed(u + 3):
                    if s.within(-3, -2):
                        pool.wait_ge(r_done, 1)
                    gather(s + 3)
                if routed(u - 3):
                    scatter(s - 3)
                if routed(u - 2):
                    scatter_index(s - 2)
                if routed(u - 1):
                    v = u - 1
                    a, b = PIECE[2]
                    wait(pool, hi_ok[2], v - UNITS2 + 1)
                    pool.tensor_tensor(w_lo[v.odd][:, a:b], raw_down[:], w_hi[v.odd][:, a:b].bitcast(F32),
                                       ALU.subtract).then_inc(lo_ok[2], 1)

            def after(u):
                if u == 0:
                    pool.wait_ge(r_tiles, 1)
                    pool.wait_ge(r_weights, 1)
                    for n_, what in enumerate((trow[:], prow[:], wpart[:, 0, :], wpart[:, 1, :], wpart[:, 2, :])):
                        pool.tensor_tensor(field_of(n_ if n_ < 2 else n_ + 1), field_of(2),
                                           view(what, 0, [[1, NK], [0, SLOTS]]), ALU.mult).then_inc(r_fields, 1)

            steps(pool, step, after)


def kernel(**inputs):
    import numpy as np
    import concourse.bacc as bacc
    from concourse.bass_utils import run_bass_kernel_spmd as run

    def a(name):
        return np.asarray(inputs[name])

    x, c = a("x"), a("ctx_2048")
    x_rows = x.reshape(BATCH, TILES, 2, HD, L).transpose(1, 3, 2, 0, 4).reshape(ROWS, L)
    cc = c.reshape(BATCH, TILES, 2, HD, BLOCKS, P)[..., ::-1].transpose(1, 5, 4, 2, 3, 0)
    cc = np.concatenate([cc, cc[..., :EXT - HD, :]], axis=-2).reshape(TILES, P, BLOCKS * GROUPS * EXT)

    def up(w1, w3):
        w = np.stack([w1, w3], 1).reshape(-1, 2, INTER, BLOCKS, P)
        return w.transpose(0, 4, 3, 1, 2).reshape(-1, P, W13)

    def down(w2):
        w = np.zeros((w2.shape[0], IPAD, L), w2.dtype)
        w[:, :INTER] = w2.transpose(0, 2, 1)
        return w.reshape(-1, ICH, P, L).transpose(0, 2, 1, 3).reshape(-1, P, W2)

    sw1, sw3 = (a("L0_ffn_" + n).reshape(SHARED, INTER, L) for n in ("sw1", "sw3"))
    sw2 = a("L0_ffn_sw2").reshape(L, SHARED, INTER).transpose(1, 0, 2)
    routed = np.concatenate([up(a("L0_ffn_w1"), a("L0_ffn_w3")), down(a("L0_ffn_w2"))], 2)
    shared = np.concatenate([up(sw1, sw3), down(sw2)], 2)
    shared = shared.transpose(1, 0, 2).reshape(P, TILES, STAGE).transpose(1, 0, 2).reshape(SHARED * P, WROW)
    weights = np.concatenate([routed.reshape(EXPERTS * P, WROW), shared], 0)
    arrays = {
        "in_x": x_rows,
        "in_ctx": cc,
        "in_conv": a("L0_xattn_ssm_kernel"),
        "in_d": a("L0_xattn_D").reshape(HEADS, 1),
        "in_gates": np.broadcast_to(np.concatenate([a("g_xattn"), a("g_ffn")])[None], (P, 2)),
        "in_gate_w": a("L0_ffn_gate_w").T.reshape(BLOCKS, P, EXPERTS).transpose(1, 0, 2).reshape(P, BLOCKS * EXPERTS),
        "in_weights": weights,
    }
    arrays = {k: np.ascontiguousarray(v) for k, v in arrays.items()}
    nc = bacc.Bacc("TRN2", target_bir_lowering=False, num_devices=1)
    aps = [nc.dram_tensor(k, v.shape, mybir.dt.from_np(v.dtype), kind="ExternalInput").ap() for k, v in arrays.items()]
    aps.append(nc.dram_tensor("out_0", (ROWS, L), F32, kind="ExternalOutput").ap())
    program(nc, *aps)
    got = run(nc, [arrays], core_ids=[0]).results[0]["out_0"]
    return got.reshape(TILES, HD, 2, BATCH, L).transpose(3, 0, 2, 1, 4).reshape(BATCH, HEADS * HD, L)
```

```python
from contextlib import ExitStack

import concourse.bass as bass
from concourse import mybir

F32 = mybir.dt.float32
F32R = mybir.dt.float32r
BF16 = mybir.dt.bfloat16
I32 = mybir.dt.int32
U32 = mybir.dt.uint32
ALU = mybir.AluOpType
ACT = mybir.ActivationFunctionType
AX = mybir.AxisListType

P = 128
BATCH, HEADS, HD, L = 8, 32, 8, 512
ROWS = BATCH * HEADS * HD
TILES = ROWS // P
BLOCKS = L // P
PAIRS = HD * (HD + 1) // 2
EXT = HD + HD // 2
GROUPS = 2 * BATCH
PRODROWS = 9
ROWS_LEFT = (2, 3, 4, 5, 6, 7, 8)
PROD_STEPS = 7
EXPERTS, INTER = 16, 352
SHARED = 2
W13 = BLOCKS * 2 * INTER
ICH = (INTER + P - 1) // P
IPAD = ICH * P
W2 = ICH * L
WROW = W13 + W2
HALF = W13 // 2
W2_DVE = W13 + (ICH - 1) * L
UNITS2 = SHARED * TILES
SLOT_TILES = (2 * ROWS + EXPERTS * (P - 1)) // P
SLOTS = SLOT_TILES + 1
KV_DVE = 1280
STAGE = SHARED * WROW // TILES
EPS = 1e-5
SKIP = 1 << 20
INFO = 6
FIELDS = 6


class At:

    def __init__(self, b, a=0, i=None, n=1):
        self.a, self.b, self.i, self.n = (a, b, i, n) if i is not None else (0, b, None, 1)

    def __add__(self, k):
        return At(self.b + k, self.a, self.i, self.n)

    def __sub__(self, k):
        return self + (-k)

    def __mul__(self, k):
        return At(self.b * k, self.a * k, self.i, self.n)

    def half(self):
        assert self.a % 2 == 0
        return At(self.b // 2, self.a // 2, self.i, self.n)

    @property
    def odd(self):
        assert self.a % 2 == 0
        return self.b % 2

    def within(self, low, high):
        ends = {low <= self.b < high, low <= self.b + self.a * (self.n - 1) < high}
        assert len(ends) == 1
        return ends.pop()

    @property
    def v(self):
        return self.b if self.i is None else self.i * self.a + self.b


def wait(eng, sem, count):
    count = count if isinstance(count, At) else At(count)
    if count.i is None and count.b <= 0:
        return
    assert count.b > 0
    eng.wait_ge(sem, count.v)


def view(ap, offset, dims):
    return bass.AP(ap.tensor, ap.offset + offset, [list(ap.ap[0])] + dims)


def program(nc, x, ctx_ext, conv_rows, conv_d, gates, gate_w, weights, out):
    ctx = ExitStack()
    with ctx:
        def sem(name):
            return ctx.enter_context(nc.semaphore(name))

        def sem2(name):
            return [sem(name + "0"), sem(name + "1")]

        def sb(name, shape, dt=F32, stack=ctx):
            return stack.enter_context(nc.sbuf_tensor(name, shape, dt))

        def sb2(name, shape, dt=F32, stack=ctx):
            return [sb(name + "0", shape, dt, stack), sb(name + "1", shape, dt, stack)]

        kpad = nc.dram_tensor("kpad", (HEADS, 640), F32, kind="Internal").ap()
        x2_rows = nc.dram_tensor("x2_rows", (ROWS, L), F32, kind="Internal").ap()
        t_rows = nc.dram_tensor("t_rows", (ROWS, L), F32, kind="Internal").ap()
        tT_rows = nc.dram_tensor("tT_rows", (ROWS, L), F32, kind="Internal").ap()
        toeplitz = bass.AP(kpad.tensor, 0, [[2 * 640, TILES], [1, P], [640, 2], [1, L]])
        x_t = x.rearrange("(t p) l -> t p l", p=P)
        x2_t = x2_rows.rearrange("(t p) l -> t p l", p=P)
        t_t = t_rows.rearrange("(t p) l -> t p l", p=P)
        tT_t = tT_rows.rearrange("(t p) l -> t p l", p=P)
        out_t = out.rearrange("(t p) l -> t p l", p=P)

        bank = [ctx.enter_context(nc.psum_tensor(f"bank{n}", [P, 512], F32)) for n in range(8)]
        ps_conv = [[bank[0], bank[1]], [bank[2], bank[3]]]
        ps_o, ps_q, ps_t, ps_gate = bank[4], bank[5], bank[6], bank[7]
        ps_h, ps_ht, ps_y = [[bank[0], bank[1]], [bank[4], bank[5]]], bank[2], [bank[3], bank[7]]
        ps_rank, ps_total, ps_table = bank[4], bank[5], bank[7]

        ident = sb("ident", [P, P])
        small = sb("small", [P, 8])
        gts = sb("gts", [P, 2])
        ahop, hop, phop = sb("ahop", [P, 7]), sb("hop", [P, 2]), sb("phop", [P, 5])
        gw = sb("gw", [P, BLOCKS * EXPERTS])
        shared_hi = sb("shared_hi", [P, SHARED * WROW], F32R)
        shared_lo = sb("shared_lo", [P, SHARED * WROW], F32R)
        logits = sb("logits", [P, TILES * EXPERTS])
        slot_info = sb("slot_info", [P, 3 * SLOTS], I32)
        tile_info = sb("tile_info", [P, INFO * SLOTS], I32)
        gat_i = sb2("gat_i", [P, 3], I32)
        sca_i = sb2("sca_i", [P, 3], I32)

        one = ExitStack()
        cx = sb2("cx", [P, BLOCKS * GROUPS * EXT], F32, one)
        toep = sb2("toep", [P, 2 * L], F32, one)
        stage = sb2("stage", [P, STAGE], F32, one)
        toep_hi, toep_lo = sb2("toep_hi", [P, 2 * L], F32R, one), sb2("toep_lo", [P, 2 * L], F32R, one)
        tT = sb2("tT", [P, L], F32, one)
        t1 = sb2("t1", [P, L], F32, one)
        x2 = sb2("x2", [P, L], F32, one)
        st1, st2 = sb2("st1_", [P, 6], F32, one), sb2("st2_", [P, 6], F32, one)
        mv1, mv2 = sb2("mv1_", [P, 3], F32, one), sb2("mv2_", [P, 3], F32, one)
        sd1, sd2 = sb2("sd1_", [P, 2], F32, one), sb2("sd2_", [P, 2], F32, one)
        kv = sb("kv", [P, BLOCKS * GROUPS * PAIRS], F32, one)
        kv_hi = sb2("kv_hi", [P, BLOCKS * GROUPS * PAIRS], F32R, one)
        kv_lo = sb2("kv_lo", [P, BLOCKS * GROUPS * PAIRS], F32R, one)
        xt = sb2("xt", [P, L], F32, one)
        xr = sb2("xr", [P, L], F32, one)
        xn = sb2("xn", [P, L], F32, one)
        q = sb2("q", [P, BLOCKS * GROUPS * EXT], F32, one)
        prod = sb2("prod", [P, PRODROWS * P], F32, one)
        krow = sb("krow", [HEADS, 640], F32, one)
        drow = sb("drow", [HEADS, 1], F32, one)
        one.close()
        tn = sb2("tn", [P, L])
        x2in = sb2("x2in", [P, L])
        tT_hi = sb2("tT_hi", [P, L], F32R)
        tT_lo = sb2("tT_lo", [P, L], F32R)
        hid = sb2("hid", [P, IPAD])
        hT_hi = sb2("hT_hi", [P, IPAD], F32R)
        hT_lo = sb2("hT_lo", [P, IPAD], F32R)
        ys = sb2("ys", [P, L])
        w_hi = [sb("w_hi0", [P, WROW], F32R)]
        w_lo = [sb("w_lo0", [P, WROW], F32R)]
        route = ExitStack()
        io = sb("io", [P, P], F32, route)
        iob = sb("iob", [P, P], BF16, route)
        upper = sb("upper", [P, P], BF16, route)
        ones = sb("ones", [P, P], BF16, route)
        mx = sb("mx", [P, TILES, 8], F32, route)
        mi = sb("mi", [P, TILES, 8], U32, route)
        pick = sb("pick", [P, 2, TILES], F32, route)
        mask = [sb(f"mask{k}", [P, TILES, EXPERTS], F32, route) for k in range(2)]
        both = sb("both", [P, TILES, EXPERTS], BF16, route)
        lex = sb("lex", [P, TILES, EXPERTS + 1], F32, route)
        ssum = sb("ssum", [P, TILES], F32, route)
        wts = sb("wts", [P, 2, TILES], F32, route)
        wres = sb("wres", [P, 2 * TILES], F32, route)
        wpart = sb("wpart", [P, 3, 2 * TILES], BF16, route)
        cum = sb2("cum", [P, TILES, EXPERTS], F32, route)
        cmp = sb("cmp", [P, EXPERTS, TILES], F32, route)
        ntile = sb2("ntile", [P, EXPERTS], F32, route)
        ntile_own = sb("ntile_own", [P, EXPERTS], F32, route)
        slot = sb("slot", [P, 2 * TILES], F32, route)
        sloti = sb("sloti", [P, 3, 2 * TILES], I32, route)
        slotb = sb("slotb", [P, 2, 2 * TILES], BF16, route)
        prow = sb("prow", [P, 2 * TILES], BF16, route)
        trow = sb("trow", [P, 2 * TILES], BF16, route)
        place = sb("place", [P, 2 * TILES, P], BF16, route)
        field = sb("field", [P, 2 * TILES, FIELDS, SLOTS], BF16, route)
        tab = sb("tab", [P, FIELDS, SLOTS], F32, route)
        tcmp = sb("tcmp", [P, SLOTS, EXPERTS], F32, route)
        texp = sb("texp", [P, SLOTS + 1], F32, route)
        tmpf = sb("tmpf", [P, SLOTS], F32, route)
        tnum = sb("tnum", [P, SLOTS], F32, route)
        inum = sb("inum", [P, SLOTS], I32, route)
        route.close()
        w_hi.append(sb("w_hi1", [P, WROW], F32R))
        w_lo.append(sb("w_lo1", [P, WROW], F32R))
        raw = sb("raw", [P, 2 * WROW])

        gates_in = sem("gates_in")
        consts_in, kpad_in, kpad_ok, kpad_out = sem("consts_in"), sem("kpad_in"), sem("kpad_ok"), sem("kpad_out")
        setup_dve, setup_pool, gate_tanh = sem("setup_dve"), sem("setup_pool"), sem("gate_tanh")
        x_in, xr_in, ctx_in, toep_in, stage_in = (sem2(n) for n in ("x_in", "xr_in", "ctx_in", "toep_in", "stage_in"))
        stat1, std1, rstd1, xn_ok = sem("stat1"), sem("std1"), sem("rstd1"), sem("xn_ok")
        q_turned, q_ok, kv_ok = sem("q_turned"), sem("q_ok"), sem("kv_ok")
        kvh_ok, kvl_ok, kvl2_ok = sem("kvh_ok"), sem("kvl_ok"), sem("kvl2_ok")
        toeph_ok, toepl_ok = sem("toeph_ok"), sem("toepl_ok")
        conv_ok, prod_ok, summed = sem("conv_ok"), sem("prod_ok"), sem("summed")
        x2_ok, stat2, std2, rstd2, t_ok = sem("x2_ok"), sem("stat2"), sem("std2"), sem("rstd2"), sem("t_ok")
        t_turned, tT_ok, gate_ok, logits_ok = sem("t_turned"), sem("tT_ok"), sem("gate_ok"), sem("logits_ok")
        shi_ok, slo_ok = sem("shi_ok"), sem("slo_ok")
        x2_out, t_out, tT_out = sem2("x2_out"), sem2("t_out"), sem2("tT_out")
        rt, r_const, r_exp, r_count, r_table = sem("rt"), sem("r_const"), sem("r_exp"), sem("r_count"), sem("r_table")
        r_both, r_tiles, r_places, r_weights = sem("r_both"), sem("r_tiles"), sem("r_places"), sem("r_weights")
        r_fields, r_done = sem("r_fields"), sem("r_done")
        tn_in, x2_in, row_in = sem2("tn_in"), sem2("x2_in"), sem2("row_in")
        tile_turned, tTh_ok, tTl_ok = sem("tile_turned"), sem("tTh_ok"), sem("tTl_ok")
        up_ok, silu_ok, hid_ok = sem("up_ok"), sem("silu_ok"), sem("hid_ok")
        hid_turned, hTh_ok, hTl_ok, down_ok = sem("hid_turned"), sem("hTh_ok"), sem("hTl_ok"), sem("down_ok")
        y_ok, yr_ok, out_ok = sem("y_ok"), sem("yr_ok"), sem2("out_ok")
        raw_in = [sem2("rawA_in"), sem2("rawB_in"), sem2("rawC_in")]
        hi2_ok, lo2_ok = sem("hi2_ok"), sem("lo2_ok")
        hi_ok = [sem("hiA_ok"), sem("hiB_ok"), sem("hiC_ok")]
        lo_ok = [sem("loA_ok"), sem("loB_ok"), sem("loC_ok")]
        gidx_ok, sidx_ok, added, hid_zero = sem("gidx_ok"), sem("sidx_ok"), sem2("added"), sem("hid_zero")
        PIECE = [(0, HALF), (HALF, W13), (W13, WROW)]

        block = ctx.enter_context(nc.Block())

        def pairs(eng, turn):
            for t in range(3):
                turn(At(t))
            n = (TILES - 4) // 2
            with eng.Fori(0, n) as i:
                for o in (3, 4):
                    turn(At(o, 2, i, n))
            turn(At(TILES - 1))

        LOOP2 = (16, 3)
        LOOP3 = (6, 19)
        LAST = SLOT_TILES + 3
        FREE_H = 8

        def steps(eng, step, after=lambda u: None):
            for u in range(-1, LOOP2[0]):
                step(At(u))
                after(u)
            with eng.Fori(0, LOOP2[1]) as i:
                for o in range(4):
                    step(At(LOOP2[0] + o, 4, i, LOOP2[1]))
            for u in range(LOOP2[0] + 4 * LOOP2[1], UNITS2 + LOOP3[0]):
                step(At(u))
            with eng.Fori(0, LOOP3[1]) as i:
                for o in range(2):
                    step(At(UNITS2 + LOOP3[0] + o, 2, i, LOOP3[1]))
            for u in range(UNITS2 + LOOP3[0] + 2 * LOOP3[1], UNITS2 + LAST):
                step(At(u))

        def shared(u):
            return u.within(0, UNITS2)

        def routed(u):
            return u.within(UNITS2, UNITS2 + SLOT_TILES)

        def tile_of(u):
            return u.half() if shared(u) else u - TILES

        def half_of(eng, s):
            return eng.value_load(tile_info[0:1, bass.ds(s.v * INFO + 2, 1)], min_val=0, max_val=WROW)

        def wait_raw(eng, n, s):
            wait(eng, raw_in[n][(s - 1).odd], ((s + 1).half()) * 16 if not (s - 1).odd else (s.half() + 1) * 16)

        def form(eng, t):
            p = t.odd
            wait(eng, kvl_ok, t)
            wait(eng, kvl2_ok, t)
            wait(eng, ctx_in[p], (t.half() + 1) * 16)
            g, hb = BLOCKS * 2, HD * BATCH
            eng.tensor_tensor(view(kv[:], 0, [[PAIRS * BATCH, g], [hb, 4], [1, hb]]),
                              view(cx[p][:], 0, [[EXT * BATCH, g], [0, 4], [1, hb]]),
                              view(cx[p][:], 0, [[EXT * BATCH, g], [BATCH, 4], [1, hb]]),
                              ALU.mult).then_inc(kv_ok, 1)
            eng.tensor_tensor(view(kv[:], 4 * hb, [[PAIRS * BATCH, g], [1, hb // 2]]),
                              view(cx[p][:], 0, [[EXT * BATCH, g], [1, hb // 2]]),
                              view(cx[p][:], hb // 2, [[EXT * BATCH, g], [1, hb // 2]]),
                              ALU.mult).then_inc(kv_ok, 1)

        def split_toep(eng, t):
            p = t.odd
            wait(eng, toeph_ok, t + 1)
            eng.tensor_tensor(toep_lo[p][:], toep[p][:], toep_hi[p][:].bitcast(F32), ALU.subtract).then_inc(toepl_ok, 1)

        def h_bank(u):
            return ps_h[1 if u.within(FREE_H, UNITS2 + LAST) and u.odd else 0]

        def y_bank(u):
            return ps_y[0 if shared(u) else u.odd]

        def turned_at(u):
            if shared(u) and not u.odd:
                return [u.half() + 1]
            if u.within(UNITS2 - 1, UNITS2):
                return [At(TILES + 1)]
            if routed(u) and routed(u + 2):
                return [tile_of(u + 2)]
            return []

        R_PICK = 2 + 2 * TILES
        R_EXP = R_PICK + 7

        NK = 2 * TILES

        def field_of(n_):
            return view(field[:], n_ * SLOTS, [[FIELDS * SLOTS, NK], [1, SLOTS]])

        @block.sync
        def _(sp):
            sp.dma_start(cx[0][:], ctx_ext[0]).then_inc(ctx_in[0], 16)
            sp.dma_start(gts[:], gates).then_inc(gates_in, 16)
            sp.wait_ge(setup_dve, 1)
            sp.dma_start(krow[:, P - 1:P - 1 + L], conv_rows).then_inc(kpad_in, 16)
            sp.dma_start(drow[:], conv_d).then_inc(kpad_in, 16)
            sp.dma_start(xt[0][:], x_t[0]).then_inc(x_in[0], 16)
            sp.wait_ge(kpad_ok, 1)
            sp.dma_start(kpad, krow[:]).then_inc(kpad_out, 16)
            sp.wait_ge(kpad_out, 16)
            shared_t = bass.AP(weights.tensor, EXPERTS * P * WROW, [[P * STAGE, TILES], [STAGE, P], [1, STAGE]])

            def load(t, which):
                p = t.odd
                if which == "toep":
                    sp.dma_start(toep[p][:].rearrange("p (h c) -> p h c", h=2),
                                 toeplitz[bass.ds(t.v, 1)].rearrange("x p h c -> (x p) h c")).then_inc(toep_in[p], 16)
                if which == "ctx":
                    sp.dma_start(cx[p][:], ctx_ext[bass.ds(t.v, 1)].rearrange("x p c -> (x p) c")).then_inc(ctx_in[p], 16)
                if which == "x":
                    sp.dma_start(xt[p][:], x_t[bass.ds(t.v, 1)].rearrange("x p c -> (x p) c")).then_inc(x_in[p], 16)
                if which == "xr":
                    sp.dma_start(xr[p][:], x_t[bass.ds(t.v, 1)].rearrange("x p c -> (x p) c")).then_inc(xr_in[p], 16)
                if which == "stage":
                    sp.dma_start(stage[p][:],
                                 shared_t[bass.ds(t.v, 1)].rearrange("x p c -> (x p) c")).then_inc(stage_in[p], 16)

            load(At(0), "toep")
            load(At(1), "ctx")
            load(At(1), "x")
            load(At(1), "toep")
            sp.dma_start(gw[:], gate_w).then_inc(consts_in, 16)
            for t in (At(0), At(1)):
                load(t, "xr")
                load(t, "stage")

            def store(t, which):
                p = t.odd
                to, src, ready, done = {"x2": (x2_t, x2, x2_ok, x2_out), "t": (t_t, t1, t_ok, t_out),
                                        "tT": (tT_t, tT, tT_ok, tT_out)}[which]
                wait(sp, ready, t + 1)
                sp.dma_start(to[bass.ds(t.v, 1)].rearrange("x p c -> (x p) c"), src[p][:]).then_inc(done[p], 16)

            def turn(t):
                first, ahead = t.within(0, 1), not t.within(TILES - 2, TILES)
                if ahead:
                    wait(sp, kv_ok, (t + 1) * 2)
                    load(t + 2, "ctx")
                    wait(sp, toepl_ok, t + 1)
                    load(t + 2, "toep")
                    wait(sp, xn_ok, t + 1)
                    load(t + 2, "x")
                if not first:
                    store(t - 1, "x2")
                    if not t.within(TILES - 1, TILES):
                        load(t + 1, "xr")
                if ahead:
                    wait(sp, slo_ok, t + 1)
                    load(t + 2, "stage")
                if not first:
                    store(t - 1, "t")
                    store(t - 1, "tT")

            turn(At(0))
            n = (TILES - 4) // 2
            with sp.Fori(0, n) as i:
                turn(At(1, 2, i, n))
                turn(At(2, 2, i, n))
            for t in range(TILES - 3, TILES - 1):
                turn(At(t))

            def load_rows(j):
                p = j.odd
                wait(sp, tTl_ok, j - 1)
                sp.dma_start(tn[p][:], tT_t[bass.ds(j.v, 1)].rearrange("x p c -> (x p) c")).then_inc(tn_in[p], 16)
                wait(sp, y_ok, j - 1)
                sp.dma_start(x2in[p][:], x2_t[bass.ds(j.v, 1)].rearrange("x p c -> (x p) c")).then_inc(x2_in[p], 16)

            sp.wait_ge(kv_ok, 2 * TILES)
            sp.wait_ge(toepl_ok, TILES)
            for p in (0, 1):
                sp.wait_ge(tT_out[p], 16)
                sp.wait_ge(x2_out[p], 16)
            load_rows(At(0))
            load_rows(At(1))
            turn(At(TILES - 1))
            for which in ("x2", "t", "tT"):
                store(At(TILES - 1), which)
            for p in (0, 1):
                for stored in (x2_out, t_out, tT_out):
                    sp.wait_ge(stored[p], 16 * TILES // 2)

            def store_rows(j):
                p = j.odd
                wait(sp, y_ok, j + 1)
                sp.dma_start(out_t[bass.ds(j.v, 1)].rearrange("x p c -> (x p) c"), ys[p][:]).then_inc(out_ok[p], 16)

            def info(s, field, most):
                return sp.value_load(tile_info[0:1, bass.ds(s.v * INFO + field, 1)], min_val=0, max_val=most)

            LAST_ROW = (EXPERTS - 1) * P

            def load_next(s, pieces):
                row, new, half = info(s, 3, LAST_ROW), info(s, 4, 1), info(s, 5, WROW)
                for n_ in pieces:
                    a, b = PIECE[n_]
                    wait_raw(sp, n_, s)
                    wait(sp, lo_ok[n_], s)
                    if n_ == 2:
                        wait(sp, lo2_ok, s)
                    sp.dma_start(raw[:, bass.ds(half + a, b - a)], weights[bass.ds(row, P), a:b],
                                 cond=(new > 0)).then_inc(raw_in[n_][s.odd], 16)

            def step(u):
                if u.within(0, UNITS2 - 2 * 2) and u.odd:
                    load_rows((u - 1).half() + 2)
                if shared(u) and u.odd and shared(u - 3) and u.within(3, UNITS2):
                    store_rows((u - 3).half())
                if u.within(UNITS2 - 3, UNITS2 - 2):
                    sp.wait_ge(r_done, 1)
                    row = info(At(0), 0, LAST_ROW)
                    for n_ in range(3):
                        a, b = PIECE[n_]
                        sp.dma_start(raw[:, a:b], weights[bass.ds(row, P), a:b]).then_inc(raw_in[n_][1], 16)
                    load_next(At(0), (0, 1, 2))
                if routed(u) and routed(u + 2):
                    load_next(u + 1 - UNITS2, (0, 1))
                if routed(u) and routed(u - 2):
                    load_next(u - 1 - UNITS2, (2,))
                if u.within(UNITS2 + 2, UNITS2 + 3):
                    store_rows(At(TILES - 1))

            steps(sp, step)
            for p in (0, 1):
                sp.wait_ge(added[p], 16 * ((SLOT_TILES + 1 - p) // 2))
                sp.wait_ge(out_ok[p], 16 * TILES // 2)

        @block.scalar
        def _(act):
            act.wait_ge(gates_in, 16)
            act.activation(small[:, 1:3], gts[:], ACT.Tanh).then_inc(gate_tanh, 1)
            act.wait_ge(setup_dve, 3)
            act.activation(small[:, 3:4], small[:, 0:1], ACT.Sqrt)

            def std_x(t):
                wait(act, stat1, (t + 1) * 2)
                act.activation(sd1[t.odd][:, 0:1], mv1[t.odd][:, 1:2], ACT.Sqrt, bias=small[:, 0:1]).then_inc(std1, 1)

            def std_x2(t):
                wait(act, stat2, (t + 1) * 2)
                act.activation(sd2[t.odd][:, 0:1], mv2[t.odd][:, 1:2], ACT.Sqrt, bias=small[:, 0:1]).then_inc(std2, 1)

            def norm_x(t):
                p = t.odd
                wait(act, q_turned, t - 1)
                wait(act, rstd1, (t + 1) * 2)
                act.activation(xn[p][:], xt[p][:], ACT.Identity, bias=mv1[p][:, 2:3],
                               scale=sd1[p][:, 1:2]).then_inc(xn_ok, 1)

            def norm_x2(t):
                p = t.odd
                wait(act, t_out[p], t.half() * 16)
                wait(act, t_turned, t - 1)
                wait(act, rstd2, (t + 1) * 2)
                act.activation(t1[p][:], x2[p][:], ACT.Identity, bias=mv2[p][:, 2:3],
                               scale=sd2[p][:, 1:2]).then_inc(t_ok, 1)

            def q_copy(t):
                p = t.odd
                wait(act, prod_ok, (t - 1) * 4 * PROD_STEPS)
                wait(act, q_turned, t + 1)
                src = ps_q[:].rearrange("p (l c) -> p l c", l=BLOCKS)
                dst = q[p][:].rearrange("p (l c) -> p l c", l=BLOCKS)
                act.activation(dst[:, :, 0:P], src, ACT.Copy).then_inc(q_ok, 1)
                act.activation(dst[:, :, P:], src[:, :, 0:GROUPS * EXT - P], ACT.Copy).then_inc(q_ok, 1)

            def tT_copy(t):
                wait(act, t_turned, t + 1)
                wait(act, tT_out[t.odd], t.half() * 16)
                wait(act, gate_ok, t - 1)
                act.activation(tT[t.odd][:], ps_t[:], ACT.Copy).then_inc(tT_ok, 1)

            def split_toep_hi(t):
                p = t.odd
                wait(act, conv_ok, (t - 1) * 8)
                wait(act, toep_in[p], (t.half() + 1) * 16)
                act.activation(toep_hi[p][:], toep[p][:], ACT.Copy).then_inc(toeph_ok, 1)

            def split_kv_hi(t):
                p = t.odd
                wait(act, conv_ok, (t - 1) * 8)
                wait(act, kv_ok, (t + 1) * 2)
                act.activation(kv_hi[p][:], kv[:], ACT.Copy).then_inc(kvh_ok, 1)

            def split_shared(t):
                p = t.odd
                wait(act, stage_in[p], (t.half() + 1) * 16)
                act.activation(shared_hi[:, bass.ds(t.v * STAGE, STAGE)], stage[p][:], ACT.Copy).then_inc(shi_ok, 1)

            split_kv_hi(At(0))
            std_x(At(0))
            norm_x(At(0))
            split_toep_hi(At(0))
            q_copy(At(0))

            def turn(t):
                if not t.within(0, 1):
                    std_x2(t - 1)
                split_shared(t)
                if not t.within(TILES - 1, TILES):
                    split_toep_hi(t + 1)
                    split_kv_hi(t + 1)
                if not t.within(0, 1):
                    norm_x2(t - 1)
                if not t.within(TILES - 1, TILES):
                    std_x(t + 1)
                    norm_x(t + 1)
                    q_copy(t + 1)
                if not t.within(0, 1):
                    tT_copy(t - 1)

            pairs(act, turn)

            def tile_hi(j):
                if j.within(0, TILES):
                    wait(act, tn_in[j.odd], (j.half() + 1) * 16)
                    wait(act, up_ok, (j - 1) * 2)
                    act.activation(tT_hi[j.odd][:], tn[j.odd][:], ACT.Copy).then_inc(tTh_ok, 1)
                else:
                    wait(act, tile_turned, j - TILES + 1)
                    act.activation(tT_hi[j.odd][:], ps_t[:], ACT.Copy).then_inc(tTh_ok, 1)

            def step(u):
                s = u - UNITS2
                if routed(u - 3):
                    v = u - 3
                    wait(act, down_ok, v + 1)
                    wait(act, added[v.odd], (v - UNITS2).half() * 16)
                    wait(act, sidx_ok, v - UNITS2 + 1)
                    if v.within(UNITS2, UNITS2 + 2):
                        wait(act, out_ok[v.odd], 16 * TILES // 2)
                    act.activation(ys[v.odd][:], y_bank(v)[:], ACT.Copy,
                                   scale=sca_i[v.odd][:, 2:3].bitcast(F32)).then_inc(yr_ok, 1)
                if routed(u + 1):
                    v = u + 1
                    half = half_of(act, v - UNITS2)
                    for n_ in (0, 1):
                        a, b = PIECE[n_]
                        wait_raw(act, n_, v - UNITS2)
                        wait(act, up_ok, v - 1)
                        c = 1 + n_ + 2 * v.odd
                        act.activation(ahop[:, c:c + 1], ahop[:, 0:1], ACT.Copy)
                        act.activation(w_hi[v.odd][:, a:b], raw[:, bass.ds(half + a, b - a)],
                                       ACT.Copy).then_inc(hi_ok[n_], 1)
                if routed(u - 1):
                    v = u - 1
                    half = half_of(act, v - UNITS2)
                    wait_raw(act, 2, v - UNITS2)
                    wait(act, down_ok, v - 1)
                    c = 5 + v.odd
                    act.activation(ahop[:, c:c + 1], ahop[:, 0:1], ACT.Copy)
                    act.activation(w_hi[v.odd][:, W13:W2_DVE], raw[:, bass.ds(half + W13, W2_DVE - W13)],
                                   ACT.Copy).then_inc(hi_ok[2], 1)
                if shared(u) or routed(u):
                    wait(act, hid_turned, u - 1)
                    if shared(u) and u.within(0, 2):
                        wait(act, hid_zero, 2)
                    wait(act, up_ok, u + 1)
                    act.activation(hid[u.odd][:, 0:INTER], h_bank(u)[0][:, 0:INTER], ACT.Silu).then_inc(silu_ok, 1)
                v = u - 1
                if shared(v) or routed(v):
                    wait(act, down_ok, v - 1)
                    wait(act, hid_turned, v + 1)
                    act.activation(hT_hi[v.odd][:], ps_ht[:, 0:IPAD], ACT.Copy).then_inc(hTh_ok, 1)
                for j in turned_at(u):
                    tile_hi(j)

            tile_hi(At(0))
            std_x2(At(TILES - 1))
            act.activation(small[:, 4:5], small[:, 0:1], ACT.Silu)
            norm_x2(At(TILES - 1))

            def after(u):
                if u == 0:
                    tT_copy(At(TILES - 1))
                if u == 4:
                    act.wait_ge(rt, R_EXP)
                    act.activation(lex[:], lex[:], ACT.Exp).then_inc(r_exp, 1)

            steps(act, step, after)

        @block.vector
        def _(dve):
            dve.memset(krow[:], 0.0).then_inc(setup_dve, 1)
            dve.memset(small[:, 0:1], EPS).then_inc(setup_dve, 1)
            dve.memset(ahop[:], 0.0).then_inc(setup_dve, 1)
            dve.memset(hop[:], 0.0).then_inc(setup_dve, 1)
            dve.wait_ge(kpad_in, 32)
            dve.tensor_tensor(krow[:, P - 1:P], krow[:, P - 1:P], drow[:], ALU.add).then_inc(kpad_ok, 1)

            def stats(src, st, mv, ok, t):
                p = t.odd
                dve.bn_stats(st[p][:], src[p][:]).then_inc(ok, 1)
                wait(dve, ok, t * 2 + 1)
                dve.tensor_copy(hop[:, 1:2], hop[:, 0:1])
                dve.bn_aggr(mv[p][:, 0:2], st[p][:]).then_inc(ok, 1)

            def stats_x(t):
                wait(dve, x_in[t.odd], (t.half() + 1) * 16)
                stats(xt, st1, mv1, stat1, t)

            def scale_x(t):
                p = t.odd
                wait(dve, std1, t + 1)
                dve.reciprocal(sd1[p][:, 1:2], sd1[p][:, 0:1]).then_inc(rstd1, 1)
                wait(dve, rstd1, t * 2 + 1)
                dve.tensor_scalar(mv1[p][:, 2:3], mv1[p][:, 0:1], sd1[p][:, 1:2], -1.0,
                                  ALU.mult, ALU.mult).then_inc(rstd1, 1)

            def residual(t):
                p = t.odd
                wait(dve, x2_out[p], t.half() * 16)
                wait(dve, xr_in[p], (t.half() + 1) * 16)
                wait(dve, summed, (t + 1) * 4)
                dve.scalar_tensor_tensor(x2[p][:], ps_o[:], small[:, 1:2], xr[p][:],
                                         ALU.mult, ALU.add).then_inc(x2_ok, 1)
                wait(dve, x2_ok, t + 1)
                stats(x2, st2, mv2, stat2, t)

            def scale_x2(t):
                p = t.odd
                wait(dve, std2, t + 1)
                dve.reciprocal(sd2[p][:, 1:2], sd2[p][:, 0:1]).then_inc(rstd2, 1)
                wait(dve, rstd2, t * 2 + 1)
                dve.tensor_scalar(mv2[p][:, 2:3], mv2[p][:, 0:1], sd2[p][:, 1:2], -1.0,
                                  ALU.mult, ALU.mult).then_inc(rstd2, 1)

            def products(t, lb):
                par = lb % 2
                G, HB = GROUPS, HD * BATCH
                for h in range(2):
                    y = ps_conv[par][h][:]
                    qo = lb * GROUPS * EXT + h * BATCH
                    po = h * BATCH
                    qq, pp = q[t.odd][:], prod[par][:]
                    if h == 0:
                        wait(dve, summed, t * 4 + lb - 1)
                        if lb == 0:
                            wait(dve, q_ok, (t + 1) * 2)
                    wait(dve, conv_ok, t * 8 + 2 * lb + h + 1)
                    dve.tensor_tensor(view(pp, po, [[P + G, 4], [G, HD], [1, BATCH]]),
                                      view(y, 0, [[HB, 4], [BATCH, HD], [1, BATCH]]),
                                      view(qq, qo, [[0, 4], [G, HD], [1, BATCH]]), ALU.mult).then_inc(prod_ok, 1)
                    dve.tensor_tensor(view(pp, po + 5 * P, [[P, 3], [G, HD], [1, BATCH]]),
                                      view(y, HB, [[HB, 3], [BATCH, HD], [1, BATCH]]),
                                      view(qq, qo + G, [[G, 3], [G, HD], [1, BATCH]]), ALU.mult).then_inc(prod_ok, 1)
                    dve.tensor_tensor(view(pp, po + 8 * P, [[4 * G, 2], [G, 4], [1, BATCH]]),
                                      view(y, 4 * HB, [[0, 2], [BATCH, 4], [1, BATCH]]),
                                      view(qq, qo + 4 * G, [[4 * G, 2], [G, 4], [1, BATCH]]), ALU.mult).then_inc(prod_ok, 1)
                wait(dve, prod_ok, (t * 4 + lb) * PROD_STEPS + 5)
                dve.tensor_tensor(prod[par][:, 5 * P:7 * P], prod[par][:, 0:2 * P], prod[par][:, 5 * P:7 * P],
                                  ALU.add).then_inc(prod_ok, 1)

            def split_kv(t):
                wait(dve, kvh_ok, t + 1)
                dve.tensor_tensor(kv_lo[t.odd][:, 0:KV_DVE], kv[:, 0:KV_DVE], kv_hi[t.odd][:, 0:KV_DVE].bitcast(F32),
                                  ALU.subtract).then_inc(kvl_ok, 1)

            def logits_copy(t):
                wait(dve, gate_ok, t + 1)
                dve.tensor_scalar(logits[:, bass.ds(t.v * EXPERTS, EXPERTS)], ps_gate[:, 0:EXPERTS], 1.0, None,
                                  ALU.mult).then_inc(logits_ok, 1)

            form(dve, At(0))
            stats_x(At(0))
            dve.memset(prod[0][:], 0.0).then_inc(setup_dve, 1)
            scale_x(At(0))
            dve.memset(prod[1][:], 0.0).then_inc(setup_dve, 1)
            split_kv(At(0))
            split_toep(dve, At(0))
            dve.wait_ge(gate_tanh, 1)
            dve.wait_ge(setup_dve, 6)

            def turn(t):
                first, last = t.within(0, 1), t.within(TILES - 1, TILES)
                products(t, 0)
                if not first:
                    residual(t - 1)
                if not first and not t.within(1, 2):
                    logits_copy(t - 2)
                products(t, 1)
                if not first:
                    scale_x2(t - 1)
                if not last:
                    stats_x(t + 1)
                products(t, 2)
                if not last:
                    scale_x(t + 1)
                    split_kv(t + 1)
                products(t, 3)

            pairs(dve, turn)

            def tile_lo(j):
                wait(dve, tTh_ok, j + 1)
                src = tn[j.odd] if j.within(0, TILES) else ps_t
                dve.tensor_tensor(tT_lo[j.odd][:], src[:], tT_hi[j.odd][:].bitcast(F32),
                                  ALU.subtract).then_inc(tTl_ok, 1)

            tile_lo(At(0))
            logits_copy(At(TILES - 2))
            residual(At(TILES - 1))
            scale_x2(At(TILES - 1))
            dve.wait_ge(slo_ok, TILES)
            dve.wait_ge(conv_ok, 8 * TILES)
            dve.memset(hid[0][:, INTER:IPAD], 0.0).then_inc(hid_zero, 1)
            dve.memset(hid[1][:, INTER:IPAD], 0.0).then_inc(hid_zero, 1)
            dve.wait_ge(hid_zero, 2)

            def step(u):
                if routed(u + 1):
                    v = u + 1
                    half = half_of(dve, v - UNITS2)
                    for n_ in (0, 1):
                        a, b = PIECE[n_]
                        wait(dve, hi_ok[n_], v - UNITS2 + 1)
                        dve.tensor_tensor(w_lo[v.odd][:, a:b], raw[:, bass.ds(half + a, b - a)],
                                          w_hi[v.odd][:, a:b].bitcast(F32), ALU.subtract).then_inc(lo_ok[n_], 1)
                if routed(u - 1):
                    v = u - 1
                    half = half_of(dve, v - UNITS2)
                    wait_raw(dve, 2, v - UNITS2)
                    wait(dve, down_ok, v - 1)
                    dve.tensor_scalar(w_hi[v.odd][:, W2_DVE:WROW], raw[:, bass.ds(half + W2_DVE, WROW - W2_DVE)], 1.0,
                                      None, ALU.mult).then_inc(hi2_ok, 1)
                    wait(dve, hi2_ok, v - UNITS2 + 1)
                    dve.tensor_tensor(w_lo[v.odd][:, W2_DVE:WROW], raw[:, bass.ds(half + W2_DVE, WROW - W2_DVE)],
                                      w_hi[v.odd][:, W2_DVE:WROW].bitcast(F32), ALU.subtract).then_inc(lo2_ok, 1)
                if shared(u) or routed(u):
                    wait(dve, silu_ok, u + 1)
                    dve.tensor_tensor(hid[u.odd][:, 0:INTER], hid[u.odd][:, 0:INTER], h_bank(u)[1][:, 0:INTER],
                                      ALU.mult).then_inc(hid_ok, 1)
                v = u - 1
                if shared(v) or routed(v):
                    wait(dve, hTh_ok, v + 1)
                    dve.tensor_tensor(hT_lo[v.odd][:], ps_ht[:, 0:IPAD], hT_hi[v.odd][:].bitcast(F32),
                                      ALU.subtract).then_inc(hTl_ok, 1)
                for j in turned_at(u):
                    tile_lo(j)
                if u.within(3, UNITS2 + 2) and u.odd:
                    j = (u - 3).half()
                    wait(dve, x2_in[j.odd], (j.half() + 1) * 16)
                    wait(dve, out_ok[j.odd], j.half() * 16)
                    wait(dve, down_ok, (j + 1) * 2)
                    dve.scalar_tensor_tensor(ys[j.odd][:], y_bank(j * 2)[:], small[:, 2:3], x2in[j.odd][:],
                                             ALU.mult, ALU.add).then_inc(y_ok, 1)

            count = [0]

            def did(ins):
                count[0] += 1
                ins.then_inc(rt, 1)

            def chain():
                dve.wait_ge(rt, count[0])

            E_, T_ = EXPERTS, TILES

            def pick_experts(tiles):
                for t in tiles:
                    did(dve.max(mx[:, t, :], logits[:, t * E_:(t + 1) * E_]))
                chain()
                for t in tiles:
                    did(dve.max_index(mi[:, t, :], mx[:, t, :], logits[:, t * E_:(t + 1) * E_]))

            def masks():
                chain()
                assert count[0] == R_PICK
                for k in range(2):
                    did(dve.tensor_copy(pick[:, k, :], mi[:, :, k]))
                chain()
                for k in range(2):
                    did(dve.tensor_tensor(mask[k][:], view(io[:], 0, [[0, T_], [1, E_]]),
                                          view(pick[:, k, :], 0, [[1, T_], [0, E_]]), ALU.is_equal))
                did(dve.tensor_tensor(lex[:, :, 0:E_], logits[:].rearrange("p (t e) -> p t e", e=E_),
                                      view(mx[:], 0, [[8, T_], [0, E_]]), ALU.subtract))
                did(dve.tensor_tensor(lex[:, :, E_:E_ + 1], mx[:, :, 1:2], mx[:, :, 0:1], ALU.subtract))
                chain()
                did(dve.tensor_tensor(both[:], mask[0][:], mask[1][:], ALU.add))
                assert count[0] == R_EXP
                dve.wait_ge(rt, count[0])
                dve.tensor_copy(hop[:, 1:2], hop[:, 0:1]).then_inc(r_both, 1)

            def softmax_weights():
                dve.wait_ge(r_exp, 1)
                did(dve.tensor_reduce(ssum[:], lex[:, :, 0:E_], AX.X, ALU.add))
                chain()
                did(dve.reciprocal(ssum[:], ssum[:]))
                chain()
                did(dve.tensor_scalar(wts[:, 0, :], ssum[:], small[:, 2:3], None, ALU.mult))
                chain()
                did(dve.tensor_tensor(wts[:, 1, :], lex[:, :, E_], wts[:, 0, :], ALU.mult))
                chain()
                flat = wts[:].rearrange("p k t -> p (k t)")
                did(dve.tensor_copy(wpart[:, 0, :], flat))
                chain()
                did(dve.tensor_tensor(wres[:], flat, wpart[:, 0, :], ALU.subtract))
                chain()
                did(dve.tensor_copy(wpart[:, 1, :], wres[:]))
                chain()
                did(dve.tensor_tensor(wres[:], wres[:], wpart[:, 1, :], ALU.subtract))
                chain()
                dve.tensor_copy(wpart[:, 2, :], wres[:]).then_inc(r_weights, 1)

            def rows_of_experts():
                dve.wait_ge(r_count, 1)
                chain()
                did(dve.tensor_copy(cum[0][:], ps_total[:, 0:T_ * E_].rearrange("p (t e) -> p t e", e=E_)))
                for n_ in range(4):
                    d, src, dst = 1 << n_, cum[n_ % 2], cum[1 - n_ % 2]
                    chain()
                    did(dve.tensor_copy(dst[:, 0:d, :], src[:, 0:d, :]))
                    did(dve.tensor_tensor(dst[:, d:, :], src[:, d:, :], src[:, 0:T_ - d, :], ALU.add))

            def tiles_of_experts():
                chain()
                did(dve.tensor_tensor(cmp[:], view(cum[0][:, T_ - 1, :], 0, [[1, E_], [0, T_]]),
                                      view(tcmp[:], 0, [[0, E_], [1, T_]]), ALU.is_gt))
                chain()
                did(dve.tensor_reduce(ntile_own[:], cmp[:], AX.X, ALU.add))
                chain()
                did(dve.tensor_copy(ntile[0][:], ntile_own[:]))
                for n_ in range(4):
                    d, src, dst = 1 << n_, ntile[n_ % 2], ntile[1 - n_ % 2]
                    chain()
                    did(dve.tensor_copy(dst[:, 0:d], src[:, 0:d]))
                    did(dve.tensor_tensor(dst[:, d:], src[:, d:], src[:, 0:E_ - d], ALU.add))
                chain()
                did(dve.tensor_tensor(ntile[1][:], ntile[0][:], ntile_own[:], ALU.subtract))
                chain()
                did(dve.tensor_scalar(ntile[1][:], ntile[1][:], float(P), None, ALU.mult))

            def slots():
                chain()
                did(dve.tensor_copy(cum[1][:, 0, :], ntile[1][:]))
                did(dve.tensor_tensor(cum[1][:, 1:, :], cum[0][:, 0:T_ - 1, :],
                                      view(ntile[1][:], 0, [[0, T_ - 1], [1, E_]]), ALU.add))
                chain()
                did(dve.tensor_tensor(cum[0][:], ps_rank[:, 0:T_ * E_].rearrange("p (t e) -> p t e", e=E_),
                                      cum[1][:], ALU.add))
                chain()
                for k in range(2):
                    did(dve.tensor_tensor(mask[k][:], mask[k][:], cum[0][:], ALU.mult))
                chain()
                for k in range(2):
                    did(dve.tensor_reduce(slot[:, k * T_:(k + 1) * T_], mask[k][:], AX.X, ALU.add))
                chain()
                did(dve.tensor_copy(sloti[:, 0, :], slot[:]))
                chain()
                did(dve.tensor_scalar(sloti[:, 1, :], sloti[:, 0, :], 7, None, ALU.logical_shift_right))
                did(dve.tensor_scalar(sloti[:, 2, :], sloti[:, 0, :], P - 1, None, ALU.bitwise_and))
                chain()
                dve.tensor_copy(slotb[:], sloti[:, 1:3, :]).then_inc(rt, 1)
                count[0] += 1

            def tiles_of_choices():
                chain()
                dve.tensor_tensor(field_of(2), view(iob[:], 0, [[0, NK], [1, SLOTS]]),
                                  view(slotb[:, 0, :], 0, [[1, NK], [0, SLOTS]]), ALU.is_equal).then_inc(r_tiles, 1)

            def places(part):
                n, n0 = NK // 4, part * NK // 4
                dve.tensor_tensor(place[:, n0:n0 + n, :], view(iob[:], 0, [[0, n], [1, P]]),
                                  view(slotb[:, 1, :], n0, [[1, n], [0, P]]), ALU.is_equal).then_inc(r_places, 1)

            ti = tile_info[:].rearrange("p (s k) -> p s k", k=INFO)

            def expert_of_tiles():
                chain()
                did(dve.tensor_tensor(tcmp[:], view(ntile[0][:], 0, [[0, SLOTS], [1, E_]]),
                                      view(io[:], 0, [[1, SLOTS], [0, E_]]), ALU.is_le))
                chain()
                did(dve.tensor_reduce(texp[:, 1:], tcmp[:], AX.X, ALU.add))
                chain()
                did(dve.tensor_scalar(texp[:, 1:], texp[:, 1:], float(E_ - 1), float(P), ALU.min, ALU.mult))
                chain()
                did(dve.tensor_tensor(tmpf[:], texp[:, 1:], texp[:, 0:SLOTS], ALU.not_equal))
                did(dve.tensor_copy(ti[:, :, 0], texp[:, 1:]))
                chain()
                did(dve.tensor_copy(ti[:, :, 1], tmpf[:]))

            def halves_of_tiles():
                did(dve.tensor_scalar(ntile_own[:], ntile_own[:], 0.0, None, ALU.is_gt))
                chain()
                did(dve.tensor_tensor(tcmp[:], tcmp[:], view(ntile_own[:], 0, [[0, SLOTS], [1, E_]]), ALU.mult))
                chain()
                did(dve.tensor_reduce(tnum[:], tcmp[:], AX.X, ALU.add))
                chain()
                did(dve.tensor_copy(inum[:], tnum[:]))
                chain()
                did(dve.tensor_scalar(inum[:], inum[:], 1, None, ALU.bitwise_and))
                chain()
                did(dve.tensor_copy(tnum[:], inum[:]))
                chain()
                did(dve.tensor_scalar(ti[:, :, 2], tnum[:], float(WROW), None, ALU.mult))
                did(dve.tensor_scalar(ti[:, :, 5], tnum[:], -float(WROW), float(WROW), ALU.mult, ALU.add))

            def experts_behind():
                chain()
                did(dve.tensor_scalar(ntile[0][:], ntile_own[:], -64.0, 64.0, ALU.mult, ALU.add))
                did(dve.tensor_scalar(tnum[:], io[:, 0:SLOTS], float(P), None, ALU.mult))
                chain()
                did(dve.tensor_tensor(ntile[0][:], ntile[0][:], io[:, 0:E_], ALU.add))
                did(dve.tensor_tensor(tcmp[:], view(ntile[1][:], 0, [[0, SLOTS], [1, E_]]),
                                      view(tnum[:], 0, [[1, SLOTS], [0, E_]]), ALU.is_le))
                chain()
                did(dve.tensor_scalar(tcmp[:], tcmp[:], 64.0, None, ALU.mult))

            def next_experts():
                chain()
                did(dve.tensor_tensor(tcmp[:], tcmp[:], view(ntile[0][:], 0, [[0, SLOTS], [1, E_]]), ALU.add))
                chain()
                did(dve.tensor_reduce(tnum[:], tcmp[:], AX.X, ALU.min))
                chain()
                did(dve.tensor_scalar(texp[:, 1:], tnum[:], float(E_), None, ALU.is_lt))
                did(dve.tensor_scalar(ti[:, :, 3], tnum[:], float(E_ - 1), float(P), ALU.min, ALU.mult))
                chain()
                did(dve.tensor_tensor(ti[:, :, 4], texp[:, 1:], tmpf[:], ALU.mult))

            def tables():
                dve.wait_ge(r_table, 1)
                chain()
                did(dve.tensor_copy(tab[:], ps_table[:, 0:FIELDS * SLOTS].rearrange("p (f s) -> p f s", s=SLOTS)))
                chain()
                si = slot_info[:].rearrange("p (s k) -> p s k", k=3)
                sf = slot_info[:].bitcast(F32).rearrange("p (s k) -> p s k", k=3)
                did(dve.scalar_tensor_tensor(tab[:, 0, :], tab[:, 0, :], float(P), tab[:, 1, :], ALU.mult, ALU.add))
                did(dve.tensor_scalar(tab[:, 2, :], tab[:, 2, :], -float(SKIP), float(SKIP), ALU.mult, ALU.add))
                did(dve.tensor_tensor(tab[:, 4, :], tab[:, 4, :], tab[:, 5, :], ALU.add))
                chain()
                did(dve.tensor_copy(si[:, :, 0], tab[:, 0, :]))
                did(dve.tensor_tensor(tab[:, 2, :], tab[:, 2, :], tab[:, 0, :], ALU.add))
                did(dve.tensor_tensor(sf[:, :, 2], tab[:, 3, :], tab[:, 4, :], ALU.add))
                chain()
                did(dve.tensor_copy(si[:, :, 1], tab[:, 2, :]))
                chain()
                dve.tensor_copy(hop[:, 1:2], hop[:, 0:1]).then_inc(r_done, 1)

            def after(u):
                if u == 1:
                    logits_copy(At(TILES - 1))
                    dve.wait_ge(logits_ok, TILES)
                    dve.wait_ge(r_const, 1)
                    dve.memset(texp[:, 0:1], -1.0).then_inc(rt, 1)
                    count[0] += 1
                    did(dve.tensor_scalar(tcmp[:, 0, 0:T_], io[:, 0:T_], float(P), None, ALU.mult))
                    pick_experts(range(T_))
                if u == 2:
                    masks()
                if u == 4:
                    rows_of_experts()
                if u == 5:
                    tiles_of_experts()
                if u == 6:
                    slots()
                if u == 7:
                    softmax_weights()
                if u == 8:
                    tiles_of_choices()
                    places(0)
                if u == 9:
                    places(1)
                    places(2)
                if u == 10:
                    places(3)
                if u == 11:
                    expert_of_tiles()
                if u == 12:
                    halves_of_tiles()
                if u == 13:
                    experts_behind()
                if u == 14:
                    next_experts()
                if u == 15:
                    tables()

            steps(dve, step, after)

        @block.tensor
        def _(pe):
            pe.wait_ge(setup_pool, 2)

            def turn_rows(src, dst, ok):
                for c in range(BLOCKS):
                    last = pe.transpose(dst[:, c * P:(c + 1) * P], src[:, c * P:(c + 1) * P], ident[:])
                last.then_inc(ok, 1)

            def turn_q(t):
                wait(pe, q_ok, t * 2)
                wait(pe, xn_ok, t + 1)
                turn_rows(xn[t.odd], ps_q, q_turned)

            def turn_t(t):
                wait(pe, tT_ok, t)
                wait(pe, t_ok, t + 1)
                turn_rows(t1[t.odd], ps_t, t_turned)

            def gate(t):
                if t.within(0, 1):
                    pe.wait_ge(consts_in, 16)
                wait(pe, logits_ok, t)
                wait(pe, tT_ok, t + 1)
                for c in range(BLOCKS):
                    last = pe.matmul(ps_gate[:, 0:EXPERTS], tT[t.odd][:, c * P:(c + 1) * P],
                                     gw[:, c * EXPERTS:(c + 1) * EXPERTS], start=(c == 0), stop=(c == BLOCKS - 1))
                last.then_inc(gate_ok, 1)

            def conv(t, lb):
                p = t.odd
                n = BATCH * PAIRS
                for h in range(2):
                    if h == 0:
                        if lb == 0:
                            wait(pe, toepl_ok, t + 1)
                            wait(pe, kvl_ok, t + 1)
                            wait(pe, kvl2_ok, t + 1)
                        wait(pe, prod_ok, (t * 4 + lb - 1) * PROD_STEPS)
                    for mb in range(lb + 1):
                        d = lb - mb
                        o = (mb * 2 + h) * n
                        k = h * L + d * P
                        for m, (w, z) in enumerate(((toep_hi, kv_hi), (toep_hi, kv_lo), (toep_lo, kv_hi))):
                            mm = pe.matmul(ps_conv[lb % 2][h][:, 0:n], w[p][:, k:k + P], z[p][:, o:o + n],
                                           start=(mb == 0 and m == 0), stop=(mb == lb and m == 2))
                    mm.then_inc(conv_ok, 1)

            def sum_rows(t, lb):
                if lb == 0:
                    wait(pe, x2_ok, t)
                wait(pe, prod_ok, (t * 4 + lb + 1) * PROD_STEPS)
                for r in ROWS_LEFT:
                    mm = pe.matmul(ps_o[:, lb * P:(lb + 1) * P], prod[lb % 2][:, r * P:(r + 1) * P], ident[:],
                                   is_transpose=True, start=(r == ROWS_LEFT[0]), stop=(r == ROWS_LEFT[-1]))
                mm.then_inc(summed, 1)

            turn_q(At(0))

            def turn(t):
                first, last = t.within(0, 1), t.within(TILES - 1, TILES)
                conv(t, 0)
                if not first and not t.within(1, 2):
                    gate(t - 2)
                if not first:
                    sum_rows(t - 1, 3)
                conv(t, 1)
                sum_rows(t, 0)
                conv(t, 2)
                sum_rows(t, 1)
                conv(t, 3)
                if not first:
                    turn_t(t - 1)
                if not last:
                    turn_q(t + 1)
                sum_rows(t, 2)

            pairs(pe, turn)
            gate(At(TILES - 2))
            sum_rows(At(TILES - 1), 3)

            def turn_tile(j):
                wait(pe, row_in[j.odd], ((j - TILES).half() + 1) * 16)
                wait(pe, tTl_ok, j)
                turn_rows(tn[j.odd], ps_t, tile_turned)

            def parts(hi, lo, whi, wlo):
                return (hi, whi), (hi, wlo), (lo, whi)

            def up(u):
                j = tile_of(u)
                wait(pe, hid_ok, u if u.within(0, FREE_H + 1) else u - 1)
                if shared(u):
                    whi, wlo, o = shared_hi, shared_lo, u.odd * WROW
                    wait(pe, slo_ok, TILES)
                else:
                    whi, wlo, o = w_hi[u.odd], w_lo[u.odd], 0
                    wait(pe, lo_ok[0], u - UNITS2 + 1)
                    wait(pe, lo_ok[1], u - UNITS2 + 1)
                wait(pe, tTl_ok, j + 1)
                for c in range(BLOCKS):
                    for k, (a, w) in enumerate(parts(tT_hi[j.odd], tT_lo[j.odd], whi, wlo)):
                        for n_, dst in enumerate(h_bank(u)):
                            f = o + (c * 2 + n_) * INTER
                            mm = pe.matmul(dst[:, 0:INTER], a[:, c * P:(c + 1) * P], w[:, f:f + INTER],
                                           start=(c == 0 and k == 0), stop=(c == BLOCKS - 1 and k == 2))
                mm.then_inc(up_ok, 1)

            def turn_hidden(u):
                wait(pe, hTl_ok, u)
                wait(pe, hid_ok, u + 1)
                for c in range(ICH):
                    last = pe.transpose(ps_ht[:, c * P:(c + 1) * P], hid[u.odd][:, c * P:(c + 1) * P], ident[:])
                last.then_inc(hid_turned, 1)

            def down(u):
                if shared(u):
                    whi, wlo, o = shared_hi, shared_lo, u.odd * WROW + W13
                    if not u.odd:
                        wait(pe, y_ok, u.half())
                    first, last = not u.odd, bool(u.odd)
                else:
                    whi, wlo, o = w_hi[u.odd], w_lo[u.odd], W13
                    if u.within(UNITS2, UNITS2 + 2):
                        wait(pe, y_ok, TILES)
                    wait(pe, yr_ok, u - UNITS2 - 1)
                    wait(pe, lo_ok[2], u - UNITS2 + 1)
                    wait(pe, lo2_ok, u - UNITS2 + 1)
                    first = last = True
                wait(pe, hTl_ok, u + 1)
                for c in range(ICH):
                    for k, (a, w) in enumerate(parts(hT_hi[u.odd], hT_lo[u.odd], whi, wlo)):
                        mm = pe.matmul(y_bank(u)[:], a[:, c * P:(c + 1) * P], w[:, o + c * L:o + (c + 1) * L],
                                       start=(first and c == 0 and k == 0), stop=(last and c == ICH - 1 and k == 2))
                mm.then_inc(down_ok, 1)

            def step(u):
                if shared(u) or routed(u):
                    up(u)
                if shared(u - 1) or routed(u - 1):
                    turn_hidden(u - 1)
                for j in turned_at(u):
                    if not j.within(0, TILES):
                        turn_tile(j)
                if shared(u - 2) or routed(u - 2):
                    down(u - 2)

            def after(u):
                if u == 0:
                    turn_t(At(TILES - 1))
                if u == 1:
                    gate(At(TILES - 1))
                if u == 3:
                    pe.wait_ge(r_both, 1)
                    pe.wait_ge(x2_ok, TILES)
                    pe.wait_ge(q_ok, 2 * TILES)
                    n = TILES * EXPERTS
                    flat = both[:].rearrange("p t e -> p (t e)")
                    pe.matmul(ps_rank[:, 0:n], upper[:], flat, start=True, stop=True)
                    pe.matmul(ps_total[:, 0:n], ones[:], flat, start=True, stop=True).then_inc(r_count, 1)
                if u == 14:
                    pe.wait_ge(r_fields, FIELDS - 1)
                    pe.wait_ge(r_places, 4)
                    for k in range(2 * TILES):
                        mm = pe.matmul(ps_table[:, 0:FIELDS * SLOTS], place[:, k, :],
                                       field[:, k, :, :].rearrange("p f s -> p (f s)"),
                                       start=(k == 0), stop=(k == 2 * TILES - 1))
                    mm.then_inc(r_table, 1)

            steps(pe, step, after)

        @block.gpsimd
        def _(pool):
            pool.iota(slot_info[:, 0:P].bitcast(F32), [[1, P]], base=0, channel_multiplier=-1,
                      allow_small_or_imprecise_dtypes=True).then_inc(setup_pool, 1)
            pool.wait_ge(setup_pool, 1)
            pool.tensor_scalar(ident[:], slot_info[:, 0:P].bitcast(F32), 0.0, None, ALU.is_equal).then_inc(setup_pool, 1)

            def split_shared(t):
                p = t.odd
                o = t * STAGE
                wait(pool, shi_ok, t + 1)
                pool.tensor_tensor(shared_lo[:, bass.ds(o.v, STAGE)], stage[p][:],
                                   shared_hi[:, bass.ds(o.v, STAGE)].bitcast(F32), ALU.subtract).then_inc(slo_ok, 1)

            def split_kv(t):
                wait(pool, kvh_ok, t + 1)
                pool.tensor_tensor(kv_lo[t.odd][:, KV_DVE:], kv[:, KV_DVE:], kv_hi[t.odd][:, KV_DVE:].bitcast(F32),
                                   ALU.subtract).then_inc(kvl2_ok, 1)

            split_kv(At(0))

            def turn(t):
                if not t.within(TILES - 1, TILES):
                    form(pool, t + 1)
                split_shared(t)
                if t.within(0, 1):
                    pool.wait_ge(conv_ok, 1)
                if not t.within(TILES - 1, TILES):
                    split_toep(pool, t + 1)
                    split_kv(t + 1)

            pairs(pool, turn)
            pool.wait_ge(conv_ok, 8 * TILES)
            pool.wait_ge(summed, 4 * TILES)
            pool.wait_ge(gate_ok, TILES)
            pool.wait_ge(t_ok, TILES)
            for p in (0, 1):
                pool.wait_ge(x2_out[p], 16 * TILES // 2)
            pool.iota(io[:], [[1, P]], base=0, channel_multiplier=0,
                      allow_small_or_imprecise_dtypes=True).then_inc(setup_pool, 1)
            pool.iota(place[:, 0, :], [[1, P]], base=0, channel_multiplier=-1,
                      allow_small_or_imprecise_dtypes=True).then_inc(setup_pool, 1)
            pool.iota(trow[:], [[0, 2], [1, TILES]], base=0, channel_multiplier=0,
                      allow_small_or_imprecise_dtypes=True).then_inc(setup_pool, 1)
            pool.iota(prow[:], [[0, 2 * TILES]], base=0, channel_multiplier=1,
                      allow_small_or_imprecise_dtypes=True).then_inc(setup_pool, 1)
            pool.memset(ones[:], 1.0).then_inc(setup_pool, 1)
            pool.memset(phop[:], 0.0).then_inc(setup_pool, 1)
            pool.wait_ge(setup_pool, 8)
            pool.tensor_copy(iob[:], io[:]).then_inc(setup_pool, 1)
            pool.tensor_scalar(upper[:], place[:, 0, :], 0.0, None, ALU.is_gt).then_inc(setup_pool, 1)
            pool.wait_ge(setup_pool, 10)
            pool.memset(phop[:, 1:2], 0.0).then_inc(r_const, 1)

            def hold(n):
                pool.tensor_tensor(phop[:, n:n + 1], phop[:, 0:1], phop[:, 0:1], ALU.add)

            def gather(s):
                p = s.odd
                if s.within(0, 2):
                    wait(pool, tTl_ok, s + TILES - 1)
                wait(pool, tile_turned, s - 1)
                wait(pool, row_in[p], s.half() * 16)
                pool.tensor_copy(gat_i[p][:], slot_info[:, bass.ds(s.v * 3, 3)]).then_inc(gidx_ok, 1)
                wait(pool, gidx_ok, s + 1)
                hold(1 + p)
                pool.indirect_dma_start(out=tn[p][:], out_offset=None, in_=t_rows,
                                        in_offset=bass.IndirectOffsetOnAxis(ap=gat_i[p][:, 0:1], axis=0),
                                        bounds_check=ROWS - 1, oob_is_err=False).then_inc(row_in[p], 16)

            def scatter(s):
                p = s.odd
                if s.within(0, 1):
                    for k in (0, 1):
                        pool.wait_ge(out_ok[k], 16 * TILES // 2)
                wait(pool, yr_ok, s + 1)
                prev = s - 1
                if not s.within(0, 1):
                    wait(pool, added[prev.odd], (prev.half() + 1) * 16)
                hold(3 + p)
                pool.indirect_dma_start(out=out, out_offset=bass.IndirectOffsetOnAxis(ap=sca_i[p][:, 1:2], axis=0),
                                        in_=ys[p][:], in_offset=None, bounds_check=ROWS - 1, oob_is_err=False,
                                        compute_op=ALU.add).then_inc(added[p], 16)

            def scatter_index(s):
                p = s.odd
                wait(pool, added[p], s.half() * 16)
                pool.tensor_copy(sca_i[p][:], slot_info[:, bass.ds(s.v * 3, 3)]).then_inc(sidx_ok, 1)

            def step(u):
                s = u - UNITS2
                if routed(u + 3):
                    if s.within(-3, -2):
                        pool.wait_ge(r_done, 1)
                    gather(s + 3)
                if routed(u - 3):
                    scatter(s - 3)
                if routed(u - 2):
                    scatter_index(s - 2)
                if routed(u - 1):
                    v = u - 1
                    half = half_of(pool, v - UNITS2)
                    wait(pool, hi_ok[2], v - UNITS2 + 1)
                    pool.tensor_tensor(w_lo[v.odd][:, W13:W2_DVE], raw[:, bass.ds(half + W13, W2_DVE - W13)],
                                       w_hi[v.odd][:, W13:W2_DVE].bitcast(F32), ALU.subtract).then_inc(lo_ok[2], 1)

            def after(u):
                if u == 0:
                    pool.wait_ge(r_tiles, 1)
                    pool.wait_ge(r_weights, 1)
                    for n_, what in enumerate((trow[:], prow[:], wpart[:, 0, :], wpart[:, 1, :], wpart[:, 2, :])):
                        pool.tensor_tensor(field_of(n_ if n_ < 2 else n_ + 1), field_of(2),
                                           view(what, 0, [[1, NK], [0, SLOTS]]), ALU.mult).then_inc(r_fields, 1)

            steps(pool, step, after)


def kernel(**inputs):
    import numpy as np
    import concourse.bacc as bacc
    from concourse.bass_utils import run_bass_kernel_spmd as run

    def a(name):
        return np.asarray(inputs[name])

    x, c = a("x"), a("ctx_2048")
    x_rows = x.reshape(BATCH, TILES, 2, HD, L).transpose(1, 3, 2, 0, 4).reshape(ROWS, L)
    cc = c.reshape(BATCH, TILES, 2, HD, BLOCKS, P)[..., ::-1].transpose(1, 5, 4, 2, 3, 0)
    cc = np.concatenate([cc, cc[..., :EXT - HD, :]], axis=-2).reshape(TILES, P, BLOCKS * GROUPS * EXT)

    def up(w1, w3):
        w = np.stack([w1, w3], 1).reshape(-1, 2, INTER, BLOCKS, P)
        return w.transpose(0, 4, 3, 1, 2).reshape(-1, P, W13)

    def down(w2):
        w = np.zeros((w2.shape[0], IPAD, L), w2.dtype)
        w[:, :INTER] = w2.transpose(0, 2, 1)
        return w.reshape(-1, ICH, P, L).transpose(0, 2, 1, 3).reshape(-1, P, W2)

    sw1, sw3 = (a("L0_ffn_" + n).reshape(SHARED, INTER, L) for n in ("sw1", "sw3"))
    sw2 = a("L0_ffn_sw2").reshape(L, SHARED, INTER).transpose(1, 0, 2)
    routed = np.concatenate([up(a("L0_ffn_w1"), a("L0_ffn_w3")), down(a("L0_ffn_w2"))], 2)
    shared = np.concatenate([up(sw1, sw3), down(sw2)], 2)
    shared = shared.transpose(1, 0, 2).reshape(P, TILES, STAGE).transpose(1, 0, 2).reshape(SHARED * P, WROW)
    weights = np.concatenate([routed.reshape(EXPERTS * P, WROW), shared], 0)
    arrays = {
        "in_x": x_rows,
        "in_ctx": cc,
        "in_conv": a("L0_xattn_ssm_kernel"),
        "in_d": a("L0_xattn_D").reshape(HEADS, 1),
        "in_gates": np.broadcast_to(np.concatenate([a("g_xattn"), a("g_ffn")])[None], (P, 2)),
        "in_gate_w": a("L0_ffn_gate_w").T.reshape(BLOCKS, P, EXPERTS).transpose(1, 0, 2).reshape(P, BLOCKS * EXPERTS),
        "in_weights": weights,
    }
    arrays = {k: np.ascontiguousarray(v) for k, v in arrays.items()}
    nc = bacc.Bacc("TRN2", target_bir_lowering=False, num_devices=1)
    aps = [nc.dram_tensor(k, v.shape, mybir.dt.from_np(v.dtype), kind="ExternalInput").ap() for k, v in arrays.items()]
    aps.append(nc.dram_tensor("out_0", (ROWS, L), F32, kind="ExternalOutput").ap())
    program(nc, *aps)
    got = run(nc, [arrays], core_ids=[0]).results[0]["out_0"]
    return got.reshape(TILES, HD, 2, BATCH, L).transpose(3, 0, 2, 1, 4).reshape(BATCH, HEADS * HD, L)
```
